# Optimizing a Trainium2 kernel written in Bass

```python
import numpy as np
import jax
import jax.numpy as jnp

def _softmax(x, axis=-1):
    return jax.nn.softmax(x, axis=axis)

def _gelu(x):
    return jax.nn.gelu(x, approximate=True)

def _silu(x):
    return jax.nn.silu(x)

def _sigmoid(x):
    return jax.nn.sigmoid(x)

def _layernorm(x, axis=-1, eps=1e-05):
    m = jnp.mean(x, axis=axis, keepdims=True)
    v = jnp.var(x, axis=axis, keepdims=True)
    return (x - m) / jnp.sqrt(v + eps)

def _scatter_add(tgt, idx, src, axis=0):
    return tgt.at[idx].add(src)

def _segment_sum(src, seg, n):
    return jax.ops.segment_sum(src, seg, n)
kernel_name = 'mk_xattn_ffn_d2_seqx_r8_ebd86b'

def setup_inputs(seed: int=0):
    np.random.seed(seed)
    _w = jnp.asarray

    def _rec_inputs():
        import jax
        import jax.numpy as jnp
        _rk = jax.random.key(seed)
        x = 7.22e-05 + 1 * jax.random.normal(jax.random.fold_in(_rk, 1), (16, 64, 512), jnp.float32)
        _lenS = 64 - jax.random.randint(jax.random.fold_in(_rk, 7), (16,), 0, max(1, 64 // 4) + 1, jnp.int32)
        _lenS2 = 64 - jax.random.randint(jax.random.fold_in(_rk, 8), (16,), 0, max(1, 64 // 4) + 1, jnp.int32)
        _ctx_4096P = jax.random.normal(jax.random.fold_in(_rk, 11), (16, 16, 512), jnp.float32)
        _ctx_4096c = jax.random.dirichlet(jax.random.fold_in(_rk, 511), 0.3 * jnp.ones((16,), jnp.float32), (16, 64))
        _ctx_4096t = jnp.einsum('bsk,bkd->bsd', _ctx_4096c, _ctx_4096P)
        _ctx_4096t = _ctx_4096t * jax.lax.rsqrt(jnp.mean(jnp.square(_ctx_4096t)) + 1e-12) * 0.953939
        ctx_4096 = 4.13588e-05 + 0.999923 * (_ctx_4096t + 0.3 * jax.random.normal(jax.random.fold_in(_rk, 611), (16, 64, 512), jnp.float32))
        _validS = jnp.arange(64)[None, :] < _lenS[:, None]
        _validS2 = jnp.arange(64)[None, :] < _lenS2[:, None]
        _causal = jnp.tril(jnp.ones((64, 64), dtype=bool))
        mask_1x1xSxS2_bk0 = jnp.logical_not(jnp.broadcast_to(_validS2[0:1, None, None, :], (1, 1, 64, 64)))
        return (x, ctx_4096, mask_1x1xSxS2_bk0)
    x, ctx_4096, mask_1x1xSxS2_bk0 = _rec_inputs()

    def _L0_xattn_setup():
        import jax, jax.numpy as jnp
        import numpy as np
        B, T, D_MODEL = (1, 256, 512)
        NUM_Q_HEADS, NUM_KV_HEADS, KEY_SIZE = (32, 8, 128)
        ATTN_MULT = 0.08838834764831845
        MAX_ATTN_VAL = 30.0

        def rotate_half(x):
            x1, x2 = jnp.split(x, 2, axis=-1)
            return jnp.concatenate((-x2, x1), axis=-1)

        def apply_rope(x):
            b, t, h, d = x.shape
            exponents = jnp.arange(0, d, 2, dtype=jnp.float32)
            inv_freq = 1.0 / 10000.0 ** (exponents / d)
            pos = jnp.arange(t, dtype=jnp.float32)
            phase = pos[:, None] * inv_freq[None, :]
            phase = jnp.tile(phase, (1, 2))[None, :, None, :]
            return (x * jnp.cos(phase) + rotate_half(x) * jnp.sin(phase)).astype(x.dtype)
        key = jax.random.key(seed)
        ks = jax.random.split(key, 8)
        query = jax.random.normal(ks[0], (B, T, D_MODEL), dtype=jnp.float32)
        kk = jax.random.normal(ks[1], (B, T, D_MODEL), dtype=jnp.float32)
        vv = jax.random.normal(ks[2], (B, T, D_MODEL), dtype=jnp.float32)
        mask = jnp.tril(jnp.ones((T, T), dtype=bool))[None, None, :, :]
        s = 0.02
        Wq = jax.random.normal(ks[3], (D_MODEL, NUM_Q_HEADS * KEY_SIZE), dtype=jnp.float32) * s
        Wk = jax.random.normal(ks[4], (D_MODEL, NUM_KV_HEADS * KEY_SIZE), dtype=jnp.float32) * s
        Wv = jax.random.normal(ks[5], (D_MODEL, NUM_KV_HEADS * KEY_SIZE), dtype=jnp.float32) * s
        Wo = jax.random.normal(ks[6], (NUM_Q_HEADS * KEY_SIZE, D_MODEL), dtype=jnp.float32) * s
        return {'query': query, 'key': kk, 'value': vv, 'mask': mask, 'Wq': Wq, 'Wk': Wk, 'Wv': Wv, 'Wo': Wo}
    _L0_xattn_all = _L0_xattn_setup()
    _L0_xattn_in = {k: v for k, v in _L0_xattn_all.items() if k in ('Wq', 'Wk', 'Wv', 'Wo')}
    del _L0_xattn_all

    def _L0_ffn_setup():
        import jax, jax.numpy as jnp
        import numpy as np
        LORA_R = 16
        SCALE = 16.0 / np.sqrt(16.0)
        NUM_EXPERTS = 4
        TOP_K = 2
        IN_F = 512
        OUT_F = 512
        key = jax.random.key(seed)
        k_x, k_a, k_b, k_r = jax.random.split(key, 4)
        x = jax.random.normal(k_x, (2, 256, IN_F), dtype=jnp.float32)
        A = jax.random.normal(k_a, (NUM_EXPERTS, LORA_R, IN_F), dtype=jnp.float32) * (1.0 / np.sqrt(IN_F))
        B = jax.random.normal(k_b, (NUM_EXPERTS, OUT_F, LORA_R), dtype=jnp.float32) * 0.02
        Wr = jax.random.normal(k_r, (NUM_EXPERTS, IN_F), dtype=jnp.float32) * 0.02
        return {'x': x, 'A': A, 'B': B, 'Wr': Wr}
    _L0_ffn_all = _L0_ffn_setup()
    _L0_ffn_in = {k: v for k, v in _L0_ffn_all.items() if k in ('A', 'B', 'Wr')}
    del _L0_ffn_all

    def _L1_xattn_setup():
        import jax, jax.numpy as jnp
        import numpy as np
        B, Q, D = (8, 64, 512)
        CTX = 512
        H, KV, HD = (16, 4, 96)
        G = H // KV
        key = jax.random.key(seed)
        ks = jax.random.split(key, 6)
        s = 0.02
        return {'latents': jax.random.normal(ks[0], (B, Q, D), jnp.float32), 'context': jax.random.normal(ks[1], (B, CTX, D), jnp.float32), 'Wq': jax.random.normal(ks[2], (H * HD, D), jnp.float32) * s, 'Wk': jax.random.normal(ks[3], (KV * HD, D), jnp.float32) * s, 'Wv': jax.random.normal(ks[4], (KV * HD, D), jnp.float32) * s, 'Wo': jax.random.normal(ks[5], (D, H * HD), jnp.float32) * s}
    _L1_xattn_all = _L1_xattn_setup()
    _L1_xattn_in = {k: v for k, v in _L1_xattn_all.items() if k in ('Wq', 'Wk', 'Wv', 'Wo')}
    del _L1_xattn_all

    def _L1_ffn_setup():
        import jax, jax.numpy as jnp
        import numpy as np
        key = jax.random.key(seed)
        k = jax.random.split(key, 6)
        x = jax.random.normal(k[0], (4, 256, 512), jnp.float32)
        W = jax.random.normal(k[1], (512, 512), jnp.float32) * 0.02
        bias = jax.random.normal(k[2], (512,), jnp.float32) * 0.02
        A = jax.random.normal(k[3], (16, 16, 512), jnp.float32) * 0.02
        Bf = jax.random.normal(k[4], (16, 512, 16), jnp.float32) * 0.02
        coeffs = jax.random.uniform(k[5], (16,), jnp.float32)
        scales = jnp.full((16,), 0.5, jnp.float32)
        return {'x': x, 'W': W, 'bias': bias, 'A': A, 'Bf': Bf, 'coeffs': coeffs, 'scales': scales}
    _L1_ffn_all = _L1_ffn_setup()
    _L1_ffn_in = {k: v for k, v in _L1_ffn_all.items() if k in ('W', 'bias', 'A', 'Bf', 'coeffs', 'scales')}
    del _L1_ffn_all
    return {'x': x, 'ctx_4096': ctx_4096, 'mask_1x1xSxS2_bk0': mask_1x1xSxS2_bk0, 'L0_xattn_Wq': _L0_xattn_in['Wq'], 'L0_xattn_Wk': _L0_xattn_in['Wk'], 'L0_xattn_Wv': _L0_xattn_in['Wv'], 'L0_xattn_Wo': _L0_xattn_in['Wo'], 'L0_ffn_A': _L0_ffn_in['A'], 'L0_ffn_B': _L0_ffn_in['B'], 'L0_ffn_Wr': _L0_ffn_in['Wr'], 'L1_xattn_Wq': _L1_xattn_in['Wq'], 'L1_xattn_Wk': _L1_xattn_in['Wk'], 'L1_xattn_Wv': _L1_xattn_in['Wv'], 'L1_xattn_Wo': _L1_xattn_in['Wo'], 'L1_ffn_W': _L1_ffn_in['W'], 'L1_ffn_bias': _L1_ffn_in['bias'], 'L1_ffn_A': _L1_ffn_in['A'], 'L1_ffn_Bf': _L1_ffn_in['Bf'], 'L1_ffn_coeffs': _L1_ffn_in['coeffs'], 'L1_ffn_scales': _L1_ffn_in['scales']}

def reference(x, ctx_4096, mask_1x1xSxS2_bk0, L0_xattn_Wq, L0_xattn_Wk, L0_xattn_Wv, L0_xattn_Wo, L0_ffn_A, L0_ffn_B, L0_ffn_Wr, L1_xattn_Wq, L1_xattn_Wk, L1_xattn_Wv, L1_xattn_Wo, L1_ffn_W, L1_ffn_bias, L1_ffn_A, L1_ffn_Bf, L1_ffn_coeffs, L1_ffn_scales):
    import jax
    import jax.numpy as jnp

    def _L0_xattn_ref(query, key, value, mask, Wq, Wk, Wv, Wo):
        import jax, jax.numpy as jnp
        import numpy as np
        B, T, D_MODEL = (1, 256, 512)
        NUM_Q_HEADS, NUM_KV_HEADS, KEY_SIZE = (32, 8, 128)
        ATTN_MULT = 0.08838834764831845
        MAX_ATTN_VAL = 30.0

        def rotate_half(x):
            x1, x2 = jnp.split(x, 2, axis=-1)
            return jnp.concatenate((-x2, x1), axis=-1)

        def apply_rope(x):
            b, t, h, d = x.shape
            exponents = jnp.arange(0, d, 2, dtype=jnp.float32)
            inv_freq = 1.0 / 10000.0 ** (exponents / d)
            pos = jnp.arange(t, dtype=jnp.float32)
            phase = pos[:, None] * inv_freq[None, :]
            phase = jnp.tile(phase, (1, 2))[None, :, None, :]
            return (x * jnp.cos(phase) + rotate_half(x) * jnp.sin(phase)).astype(x.dtype)
        b, t, _ = query.shape
        d = KEY_SIZE
        h, kv_h = (NUM_Q_HEADS, NUM_KV_HEADS)
        g = h // kv_h
        q = (query @ Wq).reshape(b, t, h, d)
        k = (key @ Wk).reshape(b, t, kv_h, d)
        v = (value @ Wv).reshape(b, t, kv_h, d)
        q = apply_rope(q)
        k = apply_rope(k)
        q = q.reshape(b, t, kv_h, g, d)
        logits = jnp.einsum('btkgd,bTkd->bkgtT', q, k).astype(jnp.float32)
        logits = logits * ATTN_MULT
        logits = MAX_ATTN_VAL * jnp.tanh(logits / MAX_ATTN_VAL)
        m = mask[:, :, None, :, :]
        logits = jnp.where(m, logits, -1e+30)
        weights = jax.nn.softmax(logits, axis=-1).astype(query.dtype)
        attn = jnp.einsum('bkgtT,bTkd->btkgd', weights, v)
        attn = attn.reshape(b, t, h * d)
        return attn @ Wo

    def _L0_ffn_ref(x, A, B, Wr):
        import jax, jax.numpy as jnp
        import numpy as np
        LORA_R = 16
        SCALE = 16.0 / np.sqrt(16.0)
        NUM_EXPERTS = 4
        TOP_K = 2
        IN_F = 512
        OUT_F = 512
        orig_shape = x.shape
        flat = x.reshape(-1, orig_shape[-1])
        logits = flat @ Wr.T
        topk_vals, topk_idx = jax.lax.top_k(logits, TOP_K)
        T = flat.shape[0]
        neg_inf = jnp.finfo(logits.dtype).min
        sparse = jnp.full_like(logits, neg_inf)
        rows = jnp.arange(T)[:, None]
        sparse = sparse.at[rows, topk_idx].set(topk_vals)
        gates = jax.nn.softmax(sparse, axis=-1)
        mid = jnp.einsum('tf,erf->ter', flat, A)
        all_deltas = jnp.einsum('ter,eor->teo', mid, B) * SCALE
        delta = jnp.sum(gates[:, :, None] * all_deltas, axis=1)
        return delta.reshape(*orig_shape[:-1], -1)

    def _L1_xattn_ref(latents, context, Wq, Wk, Wv, Wo):
        import jax, jax.numpy as jnp
        import numpy as np
        B, Q, D = (8, 64, 512)
        CTX = 512
        H, KV, HD = (16, 4, 96)
        G = H // KV
        b, q_len, _ = latents.shape
        hidden = jnp.concatenate([context, latents], axis=1)
        s_len = hidden.shape[1]
        q = (latents @ Wq.T).reshape(b, q_len, H, HD)
        k = (hidden @ Wk.T).reshape(b, s_len, KV, HD)
        v = (hidden @ Wv.T).reshape(b, s_len, KV, HD)
        q = q.transpose(0, 2, 1, 3).reshape(b, KV, G, q_len, HD)
        k = k.transpose(0, 2, 1, 3)
        v = v.transpose(0, 2, 1, 3)
        scale = 1.0 / jnp.sqrt(jnp.asarray(HD, q.dtype))
        scores = jnp.einsum('bkgqd,bksd->bkgqs', q, k) * scale
        attn = jax.nn.softmax(scores.astype(jnp.float32), axis=-1).astype(q.dtype)
        out = jnp.einsum('bkgqs,bksd->bkgqd', attn, v)
        out = out.reshape(b, H, q_len, HD).transpose(0, 2, 1, 3).reshape(b, q_len, H * HD)
        return out @ Wo.T

    def _L1_ffn_ref(x, W, bias, A, Bf, coeffs, scales):
        import jax, jax.numpy as jnp
        import numpy as np
        out = jnp.einsum('bsd,od->bso', x, W) + bias
        xa = jnp.einsum('bsd,erd->ebsr', x, A)
        w = coeffs * scales
        upd = jnp.einsum('ebsr,eor,e->bso', xa, Bf, w)
        return out + upd
    x = x + _L0_xattn_ref(_layernorm(x, axis=-1), ctx_4096, ctx_4096, mask_1x1xSxS2_bk0, L0_xattn_Wq, L0_xattn_Wk, L0_xattn_Wv, L0_xattn_Wo)
    x = x + _L0_ffn_ref(_layernorm(x, axis=-1), L0_ffn_A, L0_ffn_B, L0_ffn_Wr)
    x = x + _L1_xattn_ref(_layernorm(x, axis=-1), ctx_4096, L1_xattn_Wq, L1_xattn_Wk, L1_xattn_Wv, L1_xattn_Wo)
    x = x + _L1_ffn_ref(_layernorm(x, axis=-1), L1_ffn_W, L1_ffn_bias, L1_ffn_A, L1_ffn_Bf, L1_ffn_coeffs, L1_ffn_scales)
    return x

_drawn_inputs = setup_inputs


def setup_inputs(seed=0):
    import zlib

    import numpy as np

    out = dict(_drawn_inputs(seed))
    spreads = {'L1_ffn_scales': (0.5, 0.6)}
    factors = {'L1_xattn_Wq': 5.701, 'L1_xattn_Wk': 5.721, 'L1_ffn_bias': 3.471, 'L1_ffn_coeffs': 3.546}
    for name, (base, spread) in spreads.items():
        noise = np.random.default_rng([zlib.crc32(name.encode()), seed]).standard_normal(out[name].shape)
        drawn = base * np.exp(spread * noise) if base else spread * noise
        out[name] = jnp.asarray(drawn.astype(out[name].dtype))
    for name, factor in factors.items():
        out[name] = (out[name] * factor).astype(out[name].dtype)
    return out
```

```python
import concourse.bass as bass
from concourse import mybir
from contextlib import ExitStack

INS = ["x", "ctxT", "mask", "rope", "ident", "lowtri", "wq0", "wk0", "wv0", "wo0", "aw", "bcat",
       "wq1", "wk1", "wv1", "wo1", "w1", "a1", "bf1", "coef", "scl", "bias"]


class Lane:

    def __init__(self):
        self.items = []
        self.passed = {}

    def wait(self, *tokens):
        for tok in tokens:
            if tok is None:
                continue
            if isinstance(tok, list):
                self.wait(*tok)
                continue
            sem, value = tok
            if self.passed.get(sem.name, 0) < value:
                self.passed[sem.name] = value
                self.items.append((None, sem, value))

    def run(self, fn, sem=None, n=1):
        self.items.append((fn, sem, n))
        if sem is not None:
            sem.count += n
            return (sem, sem.count)

    def emit(self, eng):
        for fn, sem, n in self.items:
            if fn is None:
                eng.wait_ge(sem.handle, n)
            else:
                ins = fn(eng)
                if sem is not None:
                    ins.then_inc(sem.handle, n)


class Sem:
    def __init__(self, handle, name):
        self.handle, self.name, self.count = handle, name, 0


def program(nc, a, out):
    f32 = mybir.dt.float32
    f32r = mybir.dt.float32r
    i32 = mybir.dt.int32
    u8 = mybir.dt.uint8
    ALU = mybir.AluOpType
    ACT = mybir.ActivationFunctionType
    X = mybir.AxisListType.X
    ATT = 0.08838834764831845
    CAP = 30.0
    EPS = 1e-5
    SC1 = 1.0 / 96.0 ** 0.5

    with ExitStack() as ctx:
        def sb(name, shape, dt=f32):
            return ctx.enter_context(nc.sbuf_tensor(name, shape, dt))

        def sem(name):
            return Sem(ctx.enter_context(nc.semaphore(name)), name)

        xs = sb("xs", [128, 8, 512])
        HTh = sb("HTh", [128, 4, 2, 1024], f32r)
        HTl = sb("HTl", [128, 4, 2, 1024], f32r)
        arena = sb("arena", [128, 10240])
        kT = [arena[:, s * 1024:(s + 1) * 1024] for s in range(2)]
        V0 = [arena[:, 2048 + s * 2048:2048 + (s + 1) * 2048].rearrange("p (i n) -> p i n", i=8) for s in range(2)]
        rtmp = [arena[:, 6144 + s * 512:6144 + (s + 1) * 512] for s in range(2)]
        K1 = [arena[0:96, s * 2048:(s + 1) * 2048] for s in range(2)]
        V1 = arena[:, 4096:10240].rearrange("p (b n) -> p b n", b=16)
        w1T = arena[:, 0:2048].rearrange("p (k n) -> p k n", k=4)
        qb = sb("qb", [128, 2, 1024])
        aw_sb = qb[:, 0, 0:272].rearrange("p (k n) -> p k n", k=4)
        bcat_sb = qb[0:64, 0, 512:1024]
        Eb = sb("Eb", [128, 2, 512])
        pTb = sb("pTb", [128, 2, 512])
        Oh = sb("Oh", [128, 2, 2, 512], f32r)
        Ol = sb("Ol", [128, 2, 2, 512], f32r)
        WQh = sb("WQh", [128, 4, 512], f32r)
        WQl = sb("WQl", [128, 4, 512], f32r)
        WOh = sb("WOh", [128, 4, 512], f32r)
        WOl = sb("WOl", [128, 4, 512], f32r)
        WKh = sb("WKh", [128, 512], f32r)
        WKl = sb("WKl", [128, 512], f32r)
        WVh = sb("WVh", [128, 1024], f32r)
        WVl = sb("WVl", [128, 1024], f32r)
        stage = sb("stage", [128, 4, 512])
        rope = sb("rope", [128, 2, 64])
        ident = sb("ident_sb", [128, 128])
        mask32 = sb("mask32", [128, 16], i32)
        mask8 = mask32[:, :].bitcast(u8)
        mbias = sb("mbias", [128, 64])
        many = sb("many", [128, 1])
        lowtri = sb("lowtri_sb", [128, 16])
        coef = sb("coef_sb", [128, 4])
        wcol = sb("wcol", [128, 2])
        st6 = sb("st6", [128, 8, 6])
        mv = sb("mv", [128, 8, 2])
        lnb = sb("lnb", [128, 5, 8])
        sm = sb("sm", [128, 2, 2, 8])
        lg = sb("lg", [128, 4, 4])
        g16 = sb("g16", [128, 4, 16])
        e16 = sb("e16", [128, 4, 16])
        gat = sb("gat", [128, 4, 4])
        gs = sb("gs", [128, 3, 4])
        midg = sb("midg", [128, 4, 64])
        PB = [ctx.enter_context(nc.psum_tensor(f"PB{i}", [128, 512], f32)) for i in range(8)]
        PQ, PS, PT, PA, PO = PB[0:2], PB[2], PB[3], PB[4:6], PB[6:8]

        pe, act, dve, pool, sp = Lane(), Lane(), Lane(), Lane(), Lane()

        def load(dst, src, name):
            s = sem("ld_" + name)
            return sp.run(lambda e: e.dma_start(dst, src), s, 16)

        s_stage = [sem(f"ld_stage{i}") for i in range(4)]
        stage_free = [None] * 4
        stage_at = [0]

        def stage_load(pieces):
            got = []
            for src, rows, cols in pieces:
                i = stage_at[0] % 4
                stage_at[0] += 1
                sp.wait(stage_free[i])
                dst = stage[0:rows, i, 0:cols]
                tok = sp.run(lambda e, dst=dst, src=src: e.dma_start(dst, src), s_stage[i], 16)
                got.append((i, tok))
            return got

        s_whi, s_wlo = sem("w_hi"), sem("w_lo")

        def split_weight(src, rows, cols, hi, lo, free, pool_too=False):
            (i, tok), = stage_load([(src, rows, cols)])
            piece = stage[0:rows, i, 0:cols]
            act.wait(tok, free)
            th = act.run(lambda e: e.activation(hi, piece, ACT.Copy), s_whi)
            pool.wait(tok, th, free)
            tl = pool.run(lambda e: e.tensor_tensor(lo, piece, hi.bitcast(f32), ALU.subtract), s_wlo)
            stage_free[i] = [th, tl]
            return [th, tl]

        pq_free = [None, None]
        pq_at = [0]
        po_free = [None, None]
        po_at = [0]

        def next_pq():
            i = pq_at[0] % 2
            pq_at[0] += 1
            pe.wait(pq_free[i])
            return i

        def next_po():
            i = po_at[0] % 2
            po_at[0] += 1
            pe.wait(po_free[i])
            return i

        s_mm = sem("mm_proj")

        def mm3(dst, pairs, s):
            steps = []
            for Ah, Al, Bh, Bl in pairs:
                steps += [(Ah, Bh), (Ah, Bl), (Al, Bh)]
            for n, (A, B) in enumerate(steps):
                last = n == len(steps) - 1
                tok = pe.run(lambda e, A=A, B=B, n=n, last=last: e.matmul(dst, A, B, start=(n == 0), stop=last),
                             s if last else None)
            return tok

        t_ident = load(ident[:, :], a["ident"], "ident")
        t_x = [load(xs[:, i, :], a["x"][i * 128:(i + 1) * 128, :], f"x{i}") for i in range(2)]

        cst = [arena[:, 2048 + k * 1024:2048 + (k + 1) * 1024] for k in range(4)]
        t_ctx = [load(cst[k], a["ctxT"][k * 128:(k + 1) * 128, :], f"ctx{k}") for k in range(2)]
        wk_free = [None]
        wv_free = [None]

        def load_wk(j):
            return split_weight(a["wk0"][j], 128, 512, WKh[:, :], WKl[:, :], wk_free[0])

        def load_wv(p):
            toks = []
            for c in range(2):
                cols = slice(512 * c, 512 * c + 512)
                toks += split_weight(a["wv0"][p][:, cols], 128, 512, WVh[:, cols], WVl[:, cols], wv_free[0])
            return toks

        t_ctx += [load(cst[k], a["ctxT"][k * 128:(k + 1) * 128, :], f"ctx{k}") for k in range(2, 4)]
        s_ctx, s_ctl = sem("ctx_hi"), sem("ctx_lo")
        ctx_ready = []
        for k in range(4):
            src = cst[k]
            act.wait(t_ctx[k])
            th = act.run(lambda e, k=k, src=src: e.activation(HTh[:, k, 0, :], src, ACT.Copy), s_ctx)
            dve.wait(t_ctx[k], th)
            tl = dve.run(lambda e, k=k, src=src: e.tensor_tensor(
                HTl[:, k, 0, :], src, HTh[:, k, 0, :].bitcast(f32), ALU.subtract), s_ctl)
            ctx_ready += [th, tl]
        wk_tok = load_wk(0)
        t_rope = load(rope[:, :, :], a["rope"].rearrange("p (a n) -> p a n", a=2), "rope")
        t_x += [load(xs[:, i, :], a["x"][i * 128:(i + 1) * 128, :], f"x{i}") for i in range(2, 8)]
        wv_tok = load_wv(0)
        t_mask = load(mask32[:, :], a["mask"], "mask")

        s_st, s_ln, s_xn, s_xt = sem("ln_stats"), sem("ln_rstd"), sem("ln_xn"), sem("ln_T")
        s_xh, s_xl = sem("ln_hi"), sem("ln_lo")
        eb_free = [None, None]
        ptb_free = [None, None]

        def ln_stats(i, x_tok):
            dve.wait(x_tok)
            t = dve.run(lambda e: e.bn_stats(st6[:, i, :], xs[:, i, :]), s_st)
            dve.wait(t)
            return dve.run(lambda e: e.bn_aggr(mv[:, i, :], st6[:, i, :]), s_st)

        def ln_rstd(i0, n, tok, free):
            r = slice(i0, i0 + n)
            v, y, b, c, nm = (lnb[:, m, r] for m in range(5))
            dve.wait(tok, free)
            steps = [
                lambda e: e.tensor_scalar(v, mv[:, r, 1], EPS, None, ALU.add),
                lambda e: e.tensor_scalar(y.bitcast(i32), v.bitcast(i32), -0.5, 1597463007.0, ALU.mult, ALU.add),
            ]
            for _ in range(4):
                steps += [
                    lambda e: e.scalar_tensor_tensor(b, y, -0.5, y, ALU.mult, ALU.mult),
                    lambda e: e.tensor_tensor(c, b, v, ALU.mult),
                    lambda e: e.scalar_tensor_tensor(y, c, 1.5, y, ALU.add, ALU.mult),
                ]
            steps.append(lambda e: e.scalar_tensor_tensor(nm, mv[:, r, 0], -1.0, y, ALU.mult, ALU.mult))
            for f in steps:
                t = dve.run(f, s_ln)
                dve.wait(t)
            return t

        ln_at = [0]

        def ln_xn(i, tok):
            s = ln_at[0] % 2
            ln_at[0] += 1
            act.wait(tok, eb_free[s])
            return s, act.run(lambda e: e.activation(Eb[:, s, :], xs[:, i, :], ACT.Identity,
                                                     bias=lnb[:, 4, i:i + 1], scale=lnb[:, 1, i:i + 1]), s_xn)

        def ln_T(s, tok):
            p = next_pq()
            pe.wait(tok, t_ident)
            for k in range(4):
                t = pe.run(lambda e, k=k: e.transpose(PQ[p][:, k * 128:(k + 1) * 128],
                                                      Eb[:, s, k * 128:(k + 1) * 128], ident[:, :]),
                           s_xt if k == 3 else None)
            eb_free[s] = t
            return p, t

        def ln_split(i, p, tok, free):
            src = PQ[p][:, :].rearrange("p (k t) -> p k t", k=4)
            cols = slice(128 * i, 128 * i + 128)
            act.wait(tok, free)
            th = act.run(lambda e: e.activation(HTh[:, :, 1, cols], src, ACT.Copy), s_xh)
            dve.wait(th, free)
            tl = dve.run(lambda e: e.tensor_tensor(
                HTl[:, :, 1, cols], src, HTh[:, :, 1, cols].bitcast(f32), ALU.subtract), s_xl)
            pq_free[p] = [th, tl]
            return [th, tl]

        xn_read = [None] * 8

        def layernorm(tiles, x_tok, free, rstd_free=None):
            ready = {}
            st = [ln_stats(i, x_tok[i]) for i in tiles]
            t = ln_rstd(tiles[0], len(tiles), st, rstd_free)
            for i in tiles:
                s, tn = ln_xn(i, t)
                xn_read[i] = tn
                p, tt = ln_T(s, tn)
                ready[i] = ln_split(i, p, tt, free)
            return ready

        s_ra, s_rb, s_rc, s_rq = sem("rope_cos"), sem("rope_sin"), sem("rope_sin2"), sem("rope_sum")
        rtmp_free = [None, None]
        rt_at = [0]

        def rope_out(p, tok, dst, free):
            r = rt_at[0] % 2
            rt_at[0] += 1
            src = PQ[p][:, :].rearrange("p (b t) -> p b t", b=8)
            tmp = rtmp[r].rearrange("p (b t) -> p b t", b=8)
            cos = rope[:, 0:1, :].broadcast_to([128, 8, 64])
            dve.wait(tok, free, t_rope, rtmp_free[r])
            ta = dve.run(lambda e: e.tensor_tensor(dst, src, cos, ALU.mult), s_ra)
            tb = dve.run(lambda e: e.tensor_tensor(
                tmp[0:64], src[64:128], rope[64:128, 1:2, :].broadcast_to([64, 8, 64]), ALU.mult), s_rb)
            tc = dve.run(lambda e: e.tensor_tensor(
                tmp[64:128], src[0:64], rope[0:64, 1:2, :].broadcast_to([64, 8, 64]), ALU.mult), s_rc)
            pq_free[p] = tc
            pool.wait(ta, tb, tc)
            tq = pool.run(lambda e: e.tensor_tensor(dst, dst, tmp, ALU.add), s_rq)
            rtmp_free[r] = tq
            return tq

        kt_free = [None, None]
        k_ready = {}

        def k_half(j, hf, tok):
            p = next_pq()
            pe.wait(tok, ctx_ready)
            b = slice(512 * hf, 512 * hf + 512)
            t = mm3(PQ[p][:, :], [(WKh[:, k * 128:(k + 1) * 128], WKl[:, k * 128:(k + 1) * 128],
                                   HTh[:, k, 0, b], HTl[:, k, 0, b]) for k in range(4)], s_mm)
            wk_free[0] = t
            dst = kT[j % 2][:, 512 * hf:512 * hf + 512].rearrange("p (b t) -> p b t", b=8)
            k_ready.setdefault(j, []).append(rope_out(p, t, dst, kt_free[j % 2]))

        v_free = [ctx_ready, ctx_ready]
        v_ready = {}
        s_v = sem("v_sb")

        def v_tile(pr, i, tok):
            p = next_pq()
            pe.wait(tok, ctx_ready)
            b = slice(128 * i, 128 * i + 128)
            t = mm3(PQ[p][:, 0:256], [(HTh[:, k, 0, b], HTl[:, k, 0, b],
                                       WVh[:, k * 256:(k + 1) * 256], WVl[:, k * 256:(k + 1) * 256])
                                      for k in range(4)], s_mm)
            wv_free[0] = t
            act.wait(t, v_free[pr % 2])
            tv = act.run(lambda e: e.activation(V0[pr % 2][:, i, :], PQ[p][:, 0:256], ACT.Copy), s_v)
            pq_free[p] = tv
            v_ready[(pr, i)] = tv

        wq_free = [None] * 4
        wo_free = [None] * 4
        wq_tok, wo_tok = {}, {}

        def load_wq(h):
            wq_tok[h] = split_weight(a["wq0"][h], 128, 512, WQh[:, h % 4, :], WQl[:, h % 4, :], wq_free[h % 4])

        def load_wo(h):
            wo_tok[h] = split_weight(a["wo0"][h * 128:(h + 1) * 128, :], 128, 512, WOh[:, h % 4, :],
                                     WOl[:, h % 4, :], wo_free[h % 4])

        q_free = [None, None]
        q_ready = {}
        xn_ready = {}

        def stage_a(s):
            u, hf = s // 2, s % 2
            b = slice(512 * hf, 512 * hf + 512)
            toks = []
            for n in range(2):
                h = 2 * u + n
                p = next_pq()
                pe.wait(wq_tok[h], [xn_ready[i] for i in range(4 * hf, 4 * hf + 4)])
                c = h % 4
                t = mm3(PQ[p][:, :], [(WQh[:, c, k * 128:(k + 1) * 128], WQl[:, c, k * 128:(k + 1) * 128],
                                       HTh[:, k, 1, b], HTl[:, k, 1, b]) for k in range(4)], s_mm)
                wq_free[c] = t
                dst = qb[:, s % 2, :].rearrange("p (b n t) -> p n b t", b=8, n=2)[:, n]
                toks.append(rope_out(p, t, dst, q_free[s % 2]))
            q_ready[s] = toks

        s_sc, s_tanh, s_msk, s_exp = sem("scores"), sem("tanh"), sem("masked"), sem("exp")
        s_sum, s_rec, s_nrm = sem("rowsum"), sem("rowrec"), sem("probs")
        s_tr, s_pt, s_av = sem("probsT"), sem("pT_sb"), sem("av")
        s_oh, s_ol, s_wo, s_x = sem("o_hi"), sem("o_lo"), sem("wo_ps"), sem("x_sum")
        ps_free = [None]
        pt_free = [None]
        pa_free = [None, None]
        o_free = [None, None]
        p_ready, pt_ready, o_ready = {}, {}, {}
        x_ready = {i: None for i in range(8)}
        rr_free = [None, None]

        def stage_b(s):
            u, hf = s // 2, s % 2
            j = u // 2
            pe.wait(ps_free[0], q_ready[s], k_ready[j][hf])
            for b in range(8):
                t = pe.run(lambda e, b=b: e.matmul(
                    PS[:, b * 64:(b + 1) * 64], qb[:, s % 2, b * 128:(b + 1) * 128],
                    kT[j % 2][:, 512 * hf + 64 * b:512 * hf + 64 * b + 64], start=True, stop=True),
                    s_sc if b == 7 else None)
            q_free[s % 2] = t
            if s % 4 >= 2:
                kt_free[j % 2] = t
            e2 = s % 2
            E = Eb[:, e2, :]
            E3 = E.rearrange("p (b t) -> p b t", b=8)
            act.wait(t, eb_free[e2])
            t1 = act.run(lambda e: e.activation(E, PS[:, :], ACT.Tanh, scale=ATT / CAP), s_tanh)
            ps_free[0] = t1
            dve.wait(t1, t_mb)
            t2 = dve.run(lambda e: e.scalar_tensor_tensor(
                E3, E3, many[:, 0:1], mbias[:, :].unsqueeze(1).broadcast_to([128, 8, 64]), ALU.mult, ALU.add), s_msk)
            act.wait(t2)
            t3 = act.run(lambda e: e.activation(E, E, ACT.Exp, scale=CAP), s_exp)
            dve.wait(t3, rr_free[e2])
            t4 = dve.run(lambda e: e.tensor_reduce(sm[:, e2, 0, :], E3, X, ALU.add), s_sum)
            dve.wait(t4)
            t5 = dve.run(lambda e: e.reciprocal(sm[:, e2, 1, :], sm[:, e2, 0, :]), s_rec)
            dve.wait(t5)
            t6 = dve.run(lambda e: e.tensor_tensor(
                E3, E3, sm[:, e2, 1, :].unsqueeze(2).broadcast_to([128, 8, 64]), ALU.mult), s_nrm)
            rr_free[e2] = t6
            p_ready[s] = t6

        def stage_c(s):
            e2 = s % 2
            pe.wait(pt_free[0], p_ready[s], t_ident)
            for c in range(4):
                t = pe.run(lambda e, c=c: e.transpose(PT[:, c * 128:(c + 1) * 128],
                                                      Eb[:, e2, c * 128:(c + 1) * 128], ident[:, :]),
                           s_tr if c == 3 else None)
            eb_free[e2] = t
            act.wait(t, ptb_free[e2])
            tp = act.run(lambda e: e.activation(pTb[:, e2, :], PT[:, :], ACT.Copy), s_pt)
            pt_free[0] = tp
            pt_ready[s] = tp

        def stage_d(s):
            u, hf = s // 2, s % 2
            j = u // 2
            e2 = s % 2
            V = V0[(j // 2) % 2]
            c0 = 128 * (j % 2)
            pe.wait(pt_ready[s])
            toks = [None, None]
            for b in range(8):
                r, c = b % 2, b // 2
                pe.wait(pa_free[r], v_ready[(j // 2, 4 * hf + c)])
                t = pe.run(lambda e, r=r, c=c: e.matmul(
                    PA[r][:, c * 128:c * 128 + 128],
                    V[64 * r:64 * r + 64, 4 * hf + c, c0:c0 + 128],
                    pTb[64 * r:64 * r + 64, e2, c * 128:(c + 1) * 128], start=True, stop=True),
                    s_av if c == 3 else None)
                toks[r] = t
            ptb_free[e2] = t
            if j % 2 == 1 and s % 4 == 3:
                v_free[(j // 2) % 2] = t
            ready = []
            for w in range(2):
                src = PA[w][:, :].rearrange("p (c n t) -> p c n t", c=4, n=2)
                dh, dl = (O[:, e2, :, :].rearrange("p n (c r t) -> p c r n t", c=4, r=2)[:, :, w] for O in (Oh, Ol))
                act.wait(toks[w], o_free[e2])
                th = act.run(lambda e, dh=dh, src=src: e.activation(dh, src, ACT.Copy), s_oh)
                dve.wait(th, o_free[e2])
                tl = dve.run(lambda e, dh=dh, dl=dl, src=src: e.tensor_tensor(dl, src, dh.bitcast(f32), ALU.subtract), s_ol)
                pa_free[w] = [th, tl]
                ready.append([th, tl])
            o_ready[s] = ready

        def stage_e(s):
            u, hf = s // 2, s % 2
            e2 = s % 2
            for c in range(4):
                i = 4 * hf + c
                p = next_po()
                pe.wait(o_ready[s], wo_tok[2 * u], wo_tok[2 * u + 1])
                t = mm3(PO[p][:, :], [(Oh[:, e2, n, c * 128:(c + 1) * 128], Ol[:, e2, n, c * 128:(c + 1) * 128],
                                       WOh[:, (2 * u + n) % 4, :], WOl[:, (2 * u + n) % 4, :]) for n in range(2)], s_wo)
                dve.wait(t, x_ready[i], xn_read[i])
                tx = dve.run(lambda e, i=i, p=p: e.tensor_tensor(xs[:, i, :], xs[:, i, :], PO[p][:, :], ALU.add), s_x)
                po_free[p] = tx
                x_ready[i] = tx
            o_free[e2] = t
            for n in range(2):
                wo_free[(2 * u + n) % 4] = t

        s_mb = sem("mask_bias")
        dve.wait(t_mask)
        t = dve.run(lambda e: e.tensor_copy(mbias[:, :], mask8), s_mb)
        dve.wait(t)
        t = dve.run(lambda e: e.tensor_reduce(many[:, 0:1], mbias[:, :], X, ALU.max), s_mb)
        dve.wait(t)
        t = dve.run(lambda e: e.tensor_scalar(mbias[:, :], mbias[:, :], -1.0, 1e4, ALU.add, ALU.mult), s_mb)
        dve.wait(t)
        t_mb = dve.run(lambda e: e.tensor_scalar(mbias[:, :], mbias[:, :], many[:, 0:1], None, ALU.mult), s_mb)
        dve.wait(t_mb)

        for hf in range(2):
            k_half(0, hf, wk_tok)
        load_wq(0)
        load_wq(1)
        xn_ready.update(layernorm(range(0, 4), t_x, None))
        for i in range(8):
            v_tile(0, i, wv_tok)
        xn_ready.update(layernorm(range(4, 8), t_x, None))

        NS = 32
        for it in range(NS + 3):
            if it % 4 == 0 and it // 4 + 1 < 8:
                wk_tok = load_wk(it // 4 + 1)
            if it % 8 == 1 and it // 8 + 1 < 4:
                wv_tok = load_wv(it // 8 + 1)
            if it % 2 == 0 and it < NS:
                u = it // 2
                if u + 1 < 16:
                    load_wq(2 * u + 2)
                    load_wq(2 * u + 3)
                load_wo(2 * u)
                load_wo(2 * u + 1)
            if 0 <= it - 1 < NS:
                stage_b(it - 1)
            if 0 <= it - 2 < NS:
                stage_d(it - 2)
            if it < NS:
                stage_a(it)
            if 0 <= it - 2 < NS:
                stage_e(it - 2)
            if it % 4 in (1, 2) and it // 4 + 1 < 8:
                k_half(it // 4 + 1, it % 4 - 1, wk_tok)
            if 3 <= it % 8 <= 6 and it // 8 + 1 < 4:
                for i in range(2):
                    v_tile(it // 8 + 1, 2 * (it % 8 - 3) + i, wv_tok)
            if 0 <= it - 1 < NS:
                stage_c(it - 1)

        sp.wait(q_free[0], q_free[1])
        t_aw = load(aw_sb, a["aw"].rearrange("p (k n) -> p k n", k=4), "aw")
        t_bc = load(bcat_sb, a["bcat"], "bcat")
        t_low = load(lowtri[:, :], a["lowtri"], "lowtri")
        s_mid, s_gt, s_ge = sem("ffn_mid"), sem("ffn_gate"), sem("ffn_exp")
        s_xf, s_mg, s_mT, s_mTs, s_dl = sem("ffn_xT"), sem("ffn_mg"), sem("ffn_mgT"), sem("ffn_mgTs"), sem("ffn_delta")
        mid_free = None
        fft = [None, None]
        last_free = None
        for hf in range(2):
            tiles = range(4 * hf, 4 * hf + 4)
            st = [ln_stats(i, x_ready[i]) for i in tiles]
            t = ln_rstd(4 * hf, 4, st, None)
            mid = PS[:, 0:272].rearrange("p (i n) -> p i n", i=4)
            for c, i in enumerate(tiles):
                s, tn = ln_xn(i, t)
                xn_read[i] = tn
                p, tt = ln_T(s, tn)
                f = c % 2
                act.wait(tt, ptb_free[f])
                tf = act.run(lambda e, p=p, f=f: e.activation(pTb[:, f, :], PQ[p][:, :], ACT.Copy), s_xf)
                pq_free[p] = tf
                pe.wait(tf, t_aw, ps_free[0])
                for k in range(4):
                    tm = pe.run(lambda e, k=k, c=c, f=f: e.matmul(
                        mid[:, c, :], pTb[:, f, k * 128:(k + 1) * 128], aw_sb[:, k, :],
                        start=(k == 0), stop=(k == 3)), s_mid if k == 3 else None)
                ptb_free[f] = tm
            dve.wait(tm, t_low, last_free)
            L = lg[:, :, :]
            lj = L.unsqueeze(2).broadcast_to([128, 4, 4, 4])
            le = L.unsqueeze(3).broadcast_to([128, 4, 4, 4])
            G4 = g16[:, :, :].rearrange("p i (e j) -> p i e j", e=4)
            E4 = e16[:, :, :].rearrange("p i (e j) -> p i e j", e=4)
            low = lowtri[:, :].unsqueeze(1).broadcast_to([128, 4, 16])
            R = gat[:, :, :]

            def chain(fs, s):
                for f in fs:
                    t = dve.run(f, s)
                    dve.wait(t)
                return t

            t = chain([
                lambda e: e.tensor_copy(L, mid[:, :, 64:68]),
                lambda e: e.tensor_tensor(G4, lj, le, ALU.is_gt),
                lambda e: e.tensor_tensor(E4, lj, le, ALU.is_equal),
                lambda e: e.tensor_tensor(e16[:, :, :], e16[:, :, :], low, ALU.mult),
                lambda e: e.tensor_tensor(g16[:, :, :], g16[:, :, :], e16[:, :, :], ALU.add),
                lambda e: e.tensor_reduce(R, G4, X, ALU.add),
                lambda e: e.tensor_scalar(R, R, 2.0, None, ALU.is_lt),
                lambda e: e.tensor_reduce(gs[:, 0, :], L, X, ALU.max),
                lambda e: e.tensor_tensor(L, L, gs[:, 0, :].unsqueeze(2).broadcast_to([128, 4, 4]), ALU.subtract),
            ], s_gt)
            act.wait(t)
            t = act.run(lambda e: e.activation(L, L, ACT.Exp), s_ge)
            dve.wait(t)
            t = chain([
                lambda e: e.tensor_tensor(R, R, L, ALU.mult),
                lambda e: e.tensor_reduce(gs[:, 1, :], R, X, ALU.add),
                lambda e: e.reciprocal(gs[:, 2, :], gs[:, 1, :]),
                lambda e: e.scalar_tensor_tensor(
                    R, R, 4.0, gs[:, 2, :].unsqueeze(2).broadcast_to([128, 4, 4]), ALU.mult, ALU.mult),
            ], s_gt)
            for c in range(4):
                tg = dve.run(lambda e, c=c: e.tensor_tensor(
                    midg[:, c, :].rearrange("p (e r) -> p e r", e=4),
                    mid[:, c, 0:64].rearrange("p (e r) -> p e r", e=4),
                    gat[:, c, :].unsqueeze(2).broadcast_to([128, 4, 16]), ALU.mult), s_mg)
            ps_free[0] = tg
            pe.wait(tg, pt_free[0])
            for c in range(4):
                tt = pe.run(lambda e, c=c: e.transpose(PT[0:64, c * 128:(c + 1) * 128], midg[:, c, :], ident[:, :]),
                            s_mT if c == 3 else None)
            last_free = tt
            f = hf
            act.wait(tt, ptb_free[f])
            tp = act.run(lambda e, f=f: e.activation(pTb[0:64, f, :], PT[0:64, :], ACT.Copy), s_mTs)
            pt_free[0] = tp
            for c, i in enumerate(tiles):
                p = next_po()
                pe.wait(tp, t_bc)
                td = pe.run(lambda e, c=c, p=p, f=f: e.matmul(PO[p][:, :], pTb[0:64, f, c * 128:(c + 1) * 128],
                                                              bcat_sb, start=True, stop=True), s_dl)
                dve.wait(td, x_ready[i], xn_read[i])
                tx = dve.run(lambda e, i=i, p=p: e.tensor_tensor(xs[:, i, :], xs[:, i, :], PO[p][:, :], ALU.add), s_x)
                po_free[p] = tx
                x_ready[i] = tx
            ptb_free[f] = td
        ffn0_done = td

        w1k_tok = {}

        def load_wk1(j):
            w1k_tok[j] = split_weight(a["wk1"][j], 128, 384, WKh[:, 0:384], WKl[:, 0:384], wk_free[0])

        wv1_h = WOh[:, 0:3, :].rearrange("p a n -> p (a n)")
        wv1_l = WOl[:, 0:3, :].rearrange("p a n -> p (a n)")
        wv1_tok = []
        for c in range(3):
            wv1_tok += split_weight(a["wv1"][:, 512 * c:512 * c + 512], 128, 512,
                                    WOh[:, c, :], WOl[:, c, :], wo_free[c])
        load_wk1(0)

        def load_wq1(h):
            wq_tok[h] = split_weight(a["wq1"][h], 128, 384, WQh[:, h % 4, 0:384], WQl[:, h % 4, 0:384], wq_free[h % 4])

        def load_wo1(h):
            wo_tok[h] = split_weight(a["wo1"][h * 96:(h + 1) * 96, :], 96, 512, WOh[0:96, h % 4, :],
                                     WOl[0:96, h % 4, :], wo_free[h % 4])

        load_wq1(0)
        load_wq1(1)

        s_k1, s_v1 = sem("k1_sb"), sem("v1_sb")
        k1_free = [None, None]
        k1_ready = {}

        def k1_chunk(j, w, hf):
            p = next_pq()
            pe.wait(w1k_tok[j], ctx_ready)
            if w:
                pe.wait([xn_ready[i] for i in range(4 * hf, 4 * hf + 4)])
            b = slice(512 * hf, 512 * hf + 512)
            t = mm3(PQ[p][0:96, :], [(WKh[:, k * 96:(k + 1) * 96], WKl[:, k * 96:(k + 1) * 96],
                                      HTh[:, k, w, b], HTl[:, k, w, b]) for k in range(4)], s_mm)
            wk_free[0] = t
            src = PQ[p][0:96, :].rearrange("p (a r t) -> p a r t", a=4, r=2)
            dst = K1[j % 2].rearrange("p (a q t) -> p a q t", a=8, q=4)[:, 4 * hf:4 * hf + 4]
            dst = dst[:, :, 1:3, :] if w else dst[:, :, 0:4:3, :]
            act.wait(t, k1_free[j % 2])
            tk = act.run(lambda e: e.activation(dst, src, ACT.Copy), s_k1)
            pq_free[p] = tk
            k1_ready[(j, w, hf)] = tk

        v1_ready = {}

        def v1_tile(w, i):
            p = next_pq()
            pe.wait(wv1_tok, ctx_ready)
            if w:
                pe.wait(xn_ready[i])
            b = slice(128 * i, 128 * i + 128)
            t = mm3(PQ[p][:, 0:384], [(HTh[:, k, w, b], HTl[:, k, w, b],
                                       wv1_h[:, k * 384:(k + 1) * 384], wv1_l[:, k * 384:(k + 1) * 384])
                                      for k in range(4)], s_mm)
            for c in range(3):
                wo_free[c] = t
            act.wait(t)
            for r in range(2):
                at = 64 * (w ^ r)
                tv = act.run(lambda e, r=r, at=at: e.activation(V1[at:at + 64, 2 * i + r, :],
                                                                PQ[p][64 * r:64 * r + 64, 0:384], ACT.Copy), s_v1)
                v1_ready[(w, 2 * i + r)] = tv
            pq_free[p] = tv

        q1_ready = {}

        def stage_a1(u, hf):
            g = 2 * u + hf
            b = slice(512 * hf, 512 * hf + 512)
            toks = []
            for n in range(2):
                h = 2 * u + n
                p = next_pq()
                c = h % 4
                pe.wait(wq_tok[h], [xn_ready[i] for i in range(4 * hf, 4 * hf + 4)])
                t = mm3(PQ[p][0:96, :], [(WQh[:, c, k * 96:(k + 1) * 96], WQl[:, c, k * 96:(k + 1) * 96],
                                          HTh[:, k, 1, b], HTl[:, k, 1, b]) for k in range(4)], s_mm)
                wq_free[c] = t
                dst = qb[0:96, g % 2, :].rearrange("p (b n t) -> p n b t", b=8, n=2)[:, n]
                src = PQ[p][0:96, :].rearrange("p (b t) -> p b t", b=8)
                act.wait(t, q_free[g % 2], ffn0_done)
                tq = act.run(lambda e, dst=dst, src=src: e.activation(dst, src, ACT.Copy, scale=SC1), s_q1)
                pq_free[p] = tq
                toks.append(tq)
            q1_ready[g] = toks

        s_q1, s_max = sem("q1_sb"), sem("rowmax")

        def stage_b1(s):
            u, qd = s // 4, s % 4
            j, g = u // 2, 2 * u + qd // 2
            e2 = s % 2
            pe.wait(ps_free[0], q1_ready[g], k1_ready[(j, 0, qd // 2)], k1_ready[(j, 1, qd // 2)])
            for bb in range(4):
                b8, b = 4 * (qd % 2) + bb, 4 * qd + bb
                t = pe.run(lambda e, bb=bb, b8=b8, b=b: e.matmul(
                    PS[:, bb * 128:(bb + 1) * 128], qb[0:96, g % 2, b8 * 128:(b8 + 1) * 128],
                    K1[j % 2][:, b * 128:(b + 1) * 128], start=True, stop=True), s_sc if bb == 3 else None)
            q_free[g % 2] = t
            if u % 2 == 1:
                k1_free[j % 2] = t
            mx, rs = sm[:, e2, 0, 0:4], sm[:, e2, 0, 4:8]
            rr = sm[:, e2, 1, 0:4]
            E3 = Eb[:, e2, :].rearrange("p (b t) -> p b t", b=4)
            dve.wait(t, rr_free[e2])
            t1 = dve.run(lambda e: e.tensor_reduce(mx, PS[:, :].rearrange("p (b t) -> p b t", b=4), X, ALU.max,
                                                   negate=True), s_max)
            act.wait(t1, eb_free[e2])
            for bb in range(4):
                t2 = act.run(lambda e, bb=bb: e.activation(
                    Eb[:, e2, bb * 128:(bb + 1) * 128], PS[:, bb * 128:(bb + 1) * 128], ACT.Exp,
                    bias=mx[:, bb:bb + 1], accum_out=rs[:, bb:bb + 1]), s_exp)
            ps_free[0] = t2
            dve.wait(t2)
            t5 = dve.run(lambda e: e.reciprocal(rr, rs), s_rec)
            dve.wait(t5)
            t6 = dve.run(lambda e: e.tensor_tensor(E3, E3, rr.unsqueeze(2).broadcast_to([128, 4, 128]), ALU.mult), s_nrm)
            rr_free[e2] = t6
            p_ready[s] = t6

        def stage_d1(s):
            u, qd = s // 4, s % 4
            j, e2 = u // 2, s % 2
            pe.wait(pt_ready[s], pa_free[e2])
            for bb in range(4):
                b = 4 * qd + bb
                pe.wait(v1_ready[(0, b)], v1_ready[(1, b)])
                t = pe.run(lambda e, bb=bb, b=b: e.matmul(
                    PA[e2][0:96, bb * 128:(bb + 1) * 128], V1[:, b, 96 * j:96 * j + 96],
                    pTb[:, e2, bb * 128:(bb + 1) * 128], start=True, stop=True), s_av if bb == 3 else None)
            ptb_free[e2] = t
            src = PA[e2][0:96, :].rearrange("p (b n t) -> p b n t", b=4, n=2)
            dh, dl = (O[0:96, e2, :, 0:256].rearrange("p n (b t) -> p b n t", b=4) for O in (Oh, Ol))
            act.wait(t, o_free[e2])
            th = act.run(lambda e: e.activation(dh, src, ACT.Copy), s_oh)
            dve.wait(th, o_free[e2])
            tl = dve.run(lambda e: e.tensor_tensor(dl, src, dh.bitcast(f32), ALU.subtract), s_ol)
            pa_free[e2] = [th, tl]
            o_ready[s] = [th, tl]

        def stage_e1(s):
            u, qd = s // 4, s % 4
            e2 = s % 2
            for c in range(2):
                i = 2 * qd + c
                p = next_po()
                pe.wait(o_ready[s], wo_tok[2 * u], wo_tok[2 * u + 1])
                t = mm3(PO[p][:, :], [(Oh[0:96, e2, n, c * 128:(c + 1) * 128], Ol[0:96, e2, n, c * 128:(c + 1) * 128],
                                       WOh[0:96, (2 * u + n) % 4, :], WOl[0:96, (2 * u + n) % 4, :])
                                      for n in range(2)], s_wo)
                dve.wait(t, x_ready[i], xn_read[i])
                tx = dve.run(lambda e, i=i, p=p: e.tensor_tensor(xs[:, i, :], xs[:, i, :], PO[p][:, :], ALU.add), s_x)
                po_free[p] = tx
                x_ready[i] = tx
            o_free[e2] = t
            for n in range(2):
                wo_free[(2 * u + n) % 4] = t

        for hf in range(2):
            k1_chunk(0, 0, hf)
        for i in range(8):
            v1_tile(0, i)
        xn_ready = {}
        for hf in range(2):
            xn_ready.update(layernorm(range(4 * hf, 4 * hf + 4), x_ready, None))
        for hf in range(2):
            k1_chunk(0, 1, hf)
        stage_a1(0, 0)
        for i in range(8):
            v1_tile(1, i)

        wq_tok, wo_tok = {0: wq_tok[0], 1: wq_tok[1]}, {}
        weff_ready = []
        s_wc, s_bw, s_we, s_wa, s_wh, s_wl = (sem("w_col"), sem("b_scaled"), sem("weff_ps"), sem("weff_sum"),
                                              sem("weff_hi"), sem("weff_lo"))

        def ffn1_weights():
            sp.wait(k1_free[0])
            t_w = load(w1T, a["w1"].rearrange("p (k n) -> p k n", k=4), "w1")
            t_c = load(coef[:, 0:2], a["coef"], "coef")
            t_s = load(coef[:, 2:4], a["scl"], "scl")
            pieces = stage_load([(a["a1"][c], 128, 512) for c in range(2)] + [(a["bf1"][c], 128, 512) for c in range(2)])
            dve.wait(t_c, t_s)
            t = dve.run(lambda e: e.tensor_tensor(wcol[:, :], coef[:, 0:2], coef[:, 2:4], ALU.mult), s_wc)
            dve.wait(t)
            tb = []
            for c in range(2):
                i, tok = pieces[2 + c]
                dve.wait(tok)
                tb.append(dve.run(lambda e, i=i, c=c: e.tensor_scalar(stage[:, i, :], stage[:, i, :], wcol[:, c:c + 1],
                                                                      None, ALU.mult), s_bw))
            for m in range(4):
                p = next_pq()
                pe.wait(tb, pieces[0][1], pieces[1][1])
                for c in range(2):
                    ia, ib = pieces[c][0], pieces[2 + c][0]
                    t = pe.run(lambda e, ia=ia, ib=ib, c=c, m=m, p=p: e.matmul(
                        PQ[p][:, :], stage[:, ia, m * 128:(m + 1) * 128], stage[:, ib, :],
                        start=(c == 0), stop=(c == 1)), s_we if c == 1 else None)
                dve.wait(t, t_w)
                ta = dve.run(lambda e, m=m, p=p: e.tensor_tensor(w1T[:, m, :], w1T[:, m, :], PQ[p][:, :], ALU.add), s_wa)
                pq_free[p] = ta
                src = w1T[:, m, :]
                dh, dl = HTh[:, m, 0, 0:512], HTl[:, m, 0, 0:512]
                act.wait(ta, wk_free[0])
                th = act.run(lambda e, dh=dh, src=src: e.activation(dh, src, ACT.Copy), s_wh)
                dve.wait(ta, th, wk_free[0])
                tl = dve.run(lambda e, dh=dh, dl=dl, src=src: e.tensor_tensor(dl, src, dh.bitcast(f32), ALU.subtract), s_wl)
                weff_ready.extend([th, tl])
            for i, _ in pieces:
                stage_free[i] = t

        N1 = 32
        for it in range(N1 + 3):
            u, qd = it // 4, it % 4
            if it < N1 and qd == 0:
                if u + 1 < 8:
                    load_wq1(2 * u + 2)
                    load_wq1(2 * u + 3)
                load_wo1(2 * u)
                load_wo1(2 * u + 1)
                if u % 2 == 0 and u // 2 + 1 < 4:
                    load_wk1(u // 2 + 1)
            if 0 <= it - 1 < N1:
                stage_b1(it - 1)
            if 0 <= it - 2 < N1:
                stage_d1(it - 2)
            nxt = it + 2
            if it % 2 == 0 and nxt < N1:
                stage_a1(nxt // 4, (nxt % 4) // 2)
            if it < N1 and u % 2 == 1 and u // 2 + 1 < 4:
                k1_chunk(u // 2 + 1, qd // 2, qd % 2)
            if 0 <= it - 2 < N1:
                stage_e1(it - 2)
            if 0 <= it - 1 < N1:
                stage_c(it - 1)
            if it == 28:
                ffn1_weights()

        biasb = stage[:, stage_at[0] % 4, :]
        (_, t_bias), = stage_load([(a["bias"], 128, 512)])
        s_xb, s_y, s_out = sem("x_bias"), sem("y_ps"), sem("out")
        outs = []
        for hf in range(2):
            tiles = range(4 * hf, 4 * hf + 4)
            ready = layernorm(tiles, x_ready, [q_free[0], q_free[1]])
            for i in tiles:
                pool.wait(t_bias, xn_read[i], x_ready[i])
                tb = pool.run(lambda e, i=i: e.tensor_tensor(xs[:, i, :], xs[:, i, :], biasb, ALU.add), s_xb)
                p = next_po()
                pe.wait(ready[i], weff_ready)
                b = slice(128 * i, 128 * i + 128)
                t = mm3(PO[p][:, :], [(HTh[:, k, 1, b], HTl[:, k, 1, b],
                                       HTh[:, k, 0, 0:512], HTl[:, k, 0, 0:512]) for k in range(4)], s_y)
                dve.wait(t, tb)
                ty = dve.run(lambda e, i=i, p=p: e.tensor_tensor(xs[:, i, :], xs[:, i, :], PO[p][:, :], ALU.add), s_x)
                po_free[p] = ty
                sp.wait(ty)
                t_out = sp.run(lambda e, i=i: e.dma_start(out[i * 128:(i + 1) * 128, :], xs[:, i, :]), s_out, 16)
        sp.wait(t_out)

        block = ctx.enter_context(nc.Block())

        @block.sync
        def _(e):
            sp.emit(e)

        @block.scalar
        def _(e):
            act.emit(e)

        @block.gpsimd
        def _(e):
            pool.emit(e)

        @block.vector
        def _(e):
            dve.emit(e)

        @block.tensor
        def _(e):
            pe.emit(e)


def kernel(**inputs):
    import numpy as np
    import concourse.bacc as bacc
    from concourse.bass_utils import run_bass_kernel_spmd as run

    g = {k: np.asarray(v) for k, v in inputs.items()}
    half = np.float32(1.0) / np.float32(10000.0) ** (np.arange(0, 128, 2, dtype=np.float32) / np.float32(128))
    phase = np.arange(64, dtype=np.float32)[None, :] * half.astype(np.float32)[:, None]
    cos, sin = np.cos(phase), np.sin(phase)
    rope = np.concatenate([np.concatenate([cos, cos], 0), np.concatenate([sin, -sin], 0)], 1)
    low = np.array([[1.0 if j < e else 0.0 for j in range(4)] for e in range(4)], np.float32).reshape(1, 16)
    pk = lambda w: w.reshape(4, 128, -1).transpose(1, 0, 2)
    heads = lambda w, n: w.reshape(4, 128, n, -1).transpose(2, 1, 0, 3).reshape(n, 128, -1)
    a = {
        "x": g["x"].reshape(1024, 512),
        "ctxT": g["ctx_4096"].reshape(1024, 512).T,
        "mask": np.concatenate([g["mask_1x1xSxS2_bk0"].reshape(64, 64)] * 2, 0).view(np.int32),
        "rope": rope.astype(np.float32),
        "ident": np.eye(128, dtype=np.float32),
        "lowtri": np.broadcast_to(low, (128, 16)),
        "wq0": heads(g["L0_xattn_Wq"], 32),
        "wk0": heads(g["L0_xattn_Wk"], 8),
        "wv0": heads(g["L0_xattn_Wv"], 4),
        "wo0": g["L0_xattn_Wo"],
        "aw": pk(np.concatenate([g["L0_ffn_A"].reshape(64, 512), g["L0_ffn_Wr"]], 0).T).reshape(128, 272),
        "bcat": g["L0_ffn_B"].transpose(0, 2, 1).reshape(64, 512),
        "wq1": heads(g["L1_xattn_Wq"].T, 16),
        "wk1": heads(g["L1_xattn_Wk"].T, 4),
        "wv1": pk(g["L1_xattn_Wv"].T).reshape(128, 1536),
        "wo1": g["L1_xattn_Wo"].T,
        "w1": pk(g["L1_ffn_W"].T).reshape(128, 2048),
        "a1": g["L1_ffn_A"].reshape(2, 128, 512),
        "bf1": g["L1_ffn_Bf"].transpose(0, 2, 1).reshape(2, 128, 512),
        "coef": np.repeat(g["L1_ffn_coeffs"], 16).reshape(2, 128).T,
        "scl": np.repeat(g["L1_ffn_scales"], 16).reshape(2, 128).T,
        "bias": np.broadcast_to(g["L1_ffn_bias"][None, :], (128, 512)),
    }
    nc = bacc.Bacc("TRN2", target_bir_lowering=False, num_devices=1)
    arrays, aps = {}, {}
    for name in INS:
        v = np.ascontiguousarray(a[name])
        arrays["in_" + name] = v
        aps[name] = nc.dram_tensor("in_" + name, v.shape, mybir.dt.from_np(v.dtype), kind="ExternalInput").ap()
    out = nc.dram_tensor("out_0", (1024, 512), mybir.dt.float32, kind="ExternalOutput").ap()
    program(nc, aps, out)
    r = run(nc, [arrays], core_ids=[0])
    return np.asarray(r.results[0]["out_0"]).reshape(16, 64, 512)
```

```python
import concourse.bass as bass
from concourse import mybir
from contextlib import ExitStack

INS = ["x", "ctxT", "mask", "rope", "ident", "lowtri", "wq0", "wk0", "wv0", "wo0", "aw", "bcat",
       "wq1", "wk1", "wv1", "wo1", "w1", "a1", "bf1", "coef", "scl", "bias"]


class Lane:

    def __init__(self):
        self.items = []
        self.passed = {}

    def wait(self, *tokens):
        for tok in tokens:
            if tok is None:
                continue
            if isinstance(tok, list):
                self.wait(*tok)
                continue
            sem, value = tok
            if self.passed.get(sem.name, 0) < value:
                self.passed[sem.name] = value
                self.items.append((None, sem, value))

    def run(self, fn, sem=None, n=1):
        self.items.append((fn, sem, n))
        if sem is not None:
            sem.count += n
            return (sem, sem.count)

    def emit(self, eng):
        for fn, sem, n in self.items:
            if fn is None:
                eng.wait_ge(sem.handle, n)
            else:
                ins = fn(eng)
                if sem is not None:
                    ins.then_inc(sem.handle, n)


class Sem:
    def __init__(self, handle, name):
        self.handle, self.name, self.count = handle, name, 0


def program(nc, a, out):
    f32 = mybir.dt.float32
    f32r = mybir.dt.float32r
    i32 = mybir.dt.int32
    u8 = mybir.dt.uint8
    ALU = mybir.AluOpType
    ACT = mybir.ActivationFunctionType
    X = mybir.AxisListType.X
    ATT = 0.08838834764831845
    CAP = 30.0
    EPS = 1e-5
    SC1 = 1.0 / 96.0 ** 0.5

    with ExitStack() as ctx:
        def sb(name, shape, dt=f32):
            return ctx.enter_context(nc.sbuf_tensor(name, shape, dt))

        def sem(name):
            return Sem(ctx.enter_context(nc.semaphore(name)), name)

        xs = sb("xs", [128, 8, 512])
        HTh = sb("HTh", [128, 4, 2, 1024], f32r)
        HTl = sb("HTl", [128, 4, 2, 1024], f32r)
        arena = sb("arena", [128, 10240])
        kT = [arena[:, s * 1024:(s + 1) * 1024] for s in range(2)]
        V0 = [arena[:, 2048 + s * 2048:2048 + (s + 1) * 2048].rearrange("p (i n) -> p i n", i=8) for s in range(2)]
        rtmp = [arena[:, 6144 + s * 512:6144 + (s + 1) * 512] for s in range(2)]
        K1 = [arena[0:96, s * 2048:(s + 1) * 2048] for s in range(2)]
        V1 = arena[:, 4096:10240].rearrange("p (b n) -> p b n", b=16)
        w1T = arena[:, 0:2048].rearrange("p (k n) -> p k n", k=4)
        qb = sb("qb", [128, 2, 2048])
        aw_sb = qb[:, 0, 0:272].rearrange("p (k n) -> p k n", k=4)
        bcat_sb = qb[0:64, 0, 512:1024]
        Eb = sb("Eb", [128, 2, 512])
        pTb = sb("pTb", [128, 2, 512])
        Oh = sb("Oh", [128, 2, 2, 512], f32r)
        Ol = sb("Ol", [128, 2, 2, 512], f32r)
        WQh = sb("WQh", [128, 3, 512], f32r)
        WQl = sb("WQl", [128, 3, 512], f32r)
        WOh = sb("WOh", [128, 3, 512], f32r)
        WOl = sb("WOl", [128, 3, 512], f32r)
        WKh = sb("WKh", [128, 512], f32r)
        WKl = sb("WKl", [128, 512], f32r)
        WVh = sb("WVh", [128, 1024], f32r)
        WVl = sb("WVl", [128, 1024], f32r)
        stage = sb("stage", [128, 4, 512])
        rope = sb("rope", [128, 2, 64])
        ident = sb("ident_sb", [128, 128])
        mask32 = sb("mask32", [128, 16], i32)
        mask8 = mask32[:, :].bitcast(u8)
        mbias = sb("mbias", [128, 64])
        many = sb("many", [128, 1])
        lowtri = sb("lowtri_sb", [128, 16])
        coef = sb("coef_sb", [128, 4])
        wcol = sb("wcol", [128, 2])
        st6 = sb("st6", [128, 8, 6])
        mv = sb("mv", [128, 8, 2])
        lnb = sb("lnb", [128, 5, 8])
        sm = sb("sm", [128, 2, 2, 8])
        small = []
        for h in range(2):
            at = 512 * h
            small.append({})
            for n, r, c in (("lg", 4, 4), ("g16", 4, 16), ("e16", 4, 16), ("gat", 4, 4), ("gs", 3, 4), ("midg", 4, 64)):
                small[h][n] = qb[:, 1, at:at + r * c].rearrange("p (r c) -> p r c", r=r)
                at += r * c
        PB = [ctx.enter_context(nc.psum_tensor(f"PB{i}", [128, 512], f32)) for i in range(8)]
        PQ, PS, PT, PA, PO = PB[0:2], PB[2], PB[3], PB[4:6], PB[6:8]

        pe, act, dve, pool, sp = Lane(), Lane(), Lane(), Lane(), Lane()

        def load(dst, src, name):
            s = sem("ld_" + name)
            return sp.run(lambda e: e.dma_start(dst, src), s, 16)

        s_stage = [sem(f"ld_stage{i}") for i in range(4)]
        stage_free = [None] * 4
        stage_at = [0]

        def stage_load(pieces):
            got = []
            for src, rows, cols in pieces:
                i = stage_at[0] % 4
                stage_at[0] += 1
                sp.wait(stage_free[i])
                dst = stage[0:rows, i, 0:cols]
                tok = sp.run(lambda e, dst=dst, src=src: e.dma_start(dst, src), s_stage[i], 16)
                got.append((i, tok))
            return got

        s_whi, s_wlo = sem("w_hi"), sem("w_lo")

        def split_weight(src, rows, cols, hi, lo, free, pool_too=False):
            (i, tok), = stage_load([(src, rows, cols)])
            piece = stage[0:rows, i, 0:cols]
            act.wait(tok, free)
            th = act.run(lambda e: e.activation(hi, piece, ACT.Copy), s_whi)
            pool.wait(tok, th, free)
            tl = pool.run(lambda e: e.tensor_tensor(lo, piece, hi.bitcast(f32), ALU.subtract), s_wlo)
            stage_free[i] = [th, tl]
            return [th, tl]

        pq_free = [None, None]
        pq_at = [0]
        po_free = [None, None]
        po_at = [0]

        def next_pq():
            i = pq_at[0] % 2
            pq_at[0] += 1
            pe.wait(pq_free[i])
            return i

        def next_po():
            i = po_at[0] % 2
            po_at[0] += 1
            pe.wait(po_free[i])
            return i

        s_mm = sem("mm_proj")

        def mm3(dst, pairs, s):
            steps = []
            for Ah, Al, Bh, Bl in pairs:
                steps += [(Ah, Bh), (Ah, Bl), (Al, Bh)]
            for n, (A, B) in enumerate(steps):
                last = n == len(steps) - 1
                tok = pe.run(lambda e, A=A, B=B, n=n, last=last: e.matmul(dst, A, B, start=(n == 0), stop=last),
                             s if last else None)
            return tok

        cst = [[arena[:, 2048 + k * 1024 + 512 * h:2048 + k * 1024 + 512 * h + 512] for h in range(2)] for k in range(4)]
        wk_free = [None]
        wv_free = [None]

        def load_wk(j):
            return split_weight(a["wk0"][j], 128, 512, WKh[:, :], WKl[:, :], wk_free[0])

        def load_wv(p):
            toks = []
            for c in range(2):
                cols = slice(512 * c, 512 * c + 512)
                toks += split_weight(a["wv0"][p][:, cols], 128, 512, WVh[:, cols], WVl[:, cols], wv_free[0])
            return toks

        s_ctx, s_ctl = sem("ctx_hi"), sem("ctx_lo")
        ctx_half = [[], []]

        def load_ctx(h):
            cols = slice(512 * h, 512 * h + 512)
            got = [load(cst[k][h], a["ctxT"][k * 128:(k + 1) * 128, cols], f"ctx{k}{h}") for k in range(4)]
            for k in range(4):
                src = cst[k][h]
                act.wait(got[k])
                th = act.run(lambda e, k=k, src=src: e.activation(HTh[:, k, 0, cols], src, ACT.Copy), s_ctx)
                dve.wait(got[k], th)
                tl = dve.run(lambda e, k=k, src=src: e.tensor_tensor(
                    HTl[:, k, 0, cols], src, HTh[:, k, 0, cols].bitcast(f32), ALU.subtract), s_ctl)
                ctx_half[h] += [th, tl]

        wk_tok = load_wk(0)
        load_ctx(0)
        wv_tok = load_wv(0)
        t_x = [load(xs[:, i, :], a["x"][i * 128:(i + 1) * 128, :], f"x{i}") for i in range(4)]
        t_ident = load(ident[:, :], a["ident"], "ident")
        t_rope = load(rope[:, :, :], a["rope"].rearrange("p (a n) -> p a n", a=2), "rope")
        load_ctx(1)
        t_x += [load(xs[:, i, :], a["x"][i * 128:(i + 1) * 128, :], f"x{i}") for i in range(4, 8)]
        ctx_ready = [ctx_half[0], ctx_half[1]]
        t_mask = load(mask32[:, :], a["mask"], "mask")

        s_st, s_ln, s_xn, s_xt = sem("ln_stats"), sem("ln_rstd"), sem("ln_xn"), sem("ln_T")
        s_xh, s_xl = sem("ln_hi"), sem("ln_lo")
        eb_free = [None, None]
        ptb_free = [None, None]

        def ln_stats(i, x_tok):
            dve.wait(x_tok)
            t = dve.run(lambda e: e.bn_stats(st6[:, i, :], xs[:, i, :]), s_st)
            dve.wait(t)
            return dve.run(lambda e: e.bn_aggr(mv[:, i, :], st6[:, i, :]), s_st)

        def ln_rstd(i0, n, tok, free):
            r = slice(i0, i0 + n)
            v, y, b, c, nm = (lnb[:, m, r] for m in range(5))
            dve.wait(tok, free)
            steps = [
                lambda e: e.tensor_scalar(v, mv[:, r, 1], EPS, None, ALU.add),
                lambda e: e.tensor_scalar(y.bitcast(i32), v.bitcast(i32), -0.5, 1597463007.0, ALU.mult, ALU.add),
            ]
            for _ in range(3):
                steps += [
                    lambda e: e.scalar_tensor_tensor(b, y, -0.5, y, ALU.mult, ALU.mult),
                    lambda e: e.tensor_tensor(c, b, v, ALU.mult),
                    lambda e: e.scalar_tensor_tensor(y, c, 1.5, y, ALU.add, ALU.mult),
                ]
            steps.append(lambda e: e.scalar_tensor_tensor(nm, mv[:, r, 0], -1.0, y, ALU.mult, ALU.mult))
            for f in steps:
                t = dve.run(f, s_ln)
                dve.wait(t)
            return t

        ln_at = [0]

        def ln_xn(i, tok):
            s = ln_at[0] % 2
            ln_at[0] += 1
            act.wait(tok, eb_free[s])
            return s, act.run(lambda e: e.activation(Eb[:, s, :], xs[:, i, :], ACT.Identity,
                                                     bias=lnb[:, 4, i:i + 1], scale=lnb[:, 1, i:i + 1]), s_xn)

        def ln_T(s, tok):
            p = next_pq()
            pe.wait(tok, t_ident)
            for k in range(4):
                t = pe.run(lambda e, k=k: e.transpose(PQ[p][:, k * 128:(k + 1) * 128],
                                                      Eb[:, s, k * 128:(k + 1) * 128], ident[:, :]),
                           s_xt if k == 3 else None)
            eb_free[s] = t
            return p, t

        def ln_split(i, p, tok, free):
            src = PQ[p][:, :].rearrange("p (k t) -> p k t", k=4)
            cols = slice(128 * i, 128 * i + 128)
            act.wait(tok, free)
            th = act.run(lambda e: e.activation(HTh[:, :, 1, cols], src, ACT.Copy), s_xh)
            dve.wait(th, free)
            tl = dve.run(lambda e: e.tensor_tensor(
                HTl[:, :, 1, cols], src, HTh[:, :, 1, cols].bitcast(f32), ALU.subtract), s_xl)
            pq_free[p] = [th, tl]
            return [th, tl]

        xn_read = [None] * 8

        def ln_prep(tiles, x_tok, free=None):
            st = [ln_stats(i, x_tok[i]) for i in tiles]
            return ln_rstd(tiles[0], len(tiles), st, free)

        def ln_apply(tiles, tok, free, ready, filler=()):
            tiles, filler = list(tiles), list(filler)
            xn = {}

            def start(i):
                xn[i] = ln_xn(i, tok)
                xn_read[i] = xn[i][1]

            for i in tiles[:2]:
                start(i)
            for n, i in enumerate(tiles):
                p, tt = ln_T(*xn[i])
                if n + 2 < len(tiles):
                    start(tiles[n + 2])
                ready[i] = ln_split(i, p, tt, free)
                if filler:
                    filler.pop(0)()
            for f in filler:
                f()

        s_ra, s_rb, s_rc, s_rq = sem("rope_cos"), sem("rope_sin"), sem("rope_sin2"), sem("rope_sum")
        rtmp_free = [None, None]
        rt_at = [0]

        def rope_out(p, tok, dst, free):
            r = rt_at[0] % 2
            rt_at[0] += 1
            src = PQ[p][:, :].rearrange("p (b t) -> p b t", b=8)
            tmp = rtmp[r].rearrange("p (b t) -> p b t", b=8)
            cos = rope[:, 0:1, :].broadcast_to([128, 8, 64])
            dve.wait(tok, free, t_rope, rtmp_free[r])
            ta = dve.run(lambda e: e.tensor_tensor(dst, src, cos, ALU.mult), s_ra)
            tb = dve.run(lambda e: e.tensor_tensor(
                tmp[0:64], src[64:128], rope[64:128, 1:2, :].broadcast_to([64, 8, 64]), ALU.mult), s_rb)
            tc = dve.run(lambda e: e.tensor_tensor(
                tmp[64:128], src[0:64], rope[0:64, 1:2, :].broadcast_to([64, 8, 64]), ALU.mult), s_rc)
            pq_free[p] = tc
            pool.wait(ta, tb, tc)
            tq = pool.run(lambda e: e.tensor_tensor(dst, dst, tmp, ALU.add), s_rq)
            rtmp_free[r] = tq
            return tq

        kt_free = [None, None]
        k_ready = {}

        def k_half(j, hf, tok):
            p = next_pq()
            pe.wait(tok, ctx_half[hf])
            b = slice(512 * hf, 512 * hf + 512)
            t = mm3(PQ[p][:, :], [(WKh[:, k * 128:(k + 1) * 128], WKl[:, k * 128:(k + 1) * 128],
                                   HTh[:, k, 0, b], HTl[:, k, 0, b]) for k in range(4)], s_mm)
            wk_free[0] = t
            dst = kT[j % 2][:, 512 * hf:512 * hf + 512].rearrange("p (b t) -> p b t", b=8)
            k_ready.setdefault(j, []).append(rope_out(p, t, dst, kt_free[j % 2]))

        v_free = [ctx_ready, ctx_ready]
        v_ready = {}
        s_v = sem("v_sb")

        def v_tile(pr, i, tok):
            p = next_pq()
            pe.wait(tok, ctx_half[i // 4])
            b = slice(128 * i, 128 * i + 128)
            t = mm3(PQ[p][:, 0:256], [(HTh[:, k, 0, b], HTl[:, k, 0, b],
                                       WVh[:, k * 256:(k + 1) * 256], WVl[:, k * 256:(k + 1) * 256])
                                      for k in range(4)], s_mm)
            wv_free[0] = t
            act.wait(t, v_free[pr % 2])
            tv = act.run(lambda e: e.activation(V0[pr % 2][:, i, :], PQ[p][:, 0:256], ACT.Copy), s_v)
            pq_free[p] = tv
            v_ready[(pr, i)] = tv

        wq_free = [None] * 3
        wo_free = [None] * 3
        wq_tok, wo_tok = {}, {}

        def load_wq(h):
            wq_tok[h] = split_weight(a["wq0"][h], 128, 512, WQh[:, h % 3, :], WQl[:, h % 3, :], wq_free[h % 3])

        def load_wo(h):
            wo_tok[h] = split_weight(a["wo0"][h * 128:(h + 1) * 128, :], 128, 512, WOh[:, h % 3, :],
                                     WOl[:, h % 3, :], wo_free[h % 3])

        q_free = [None, None]
        q_ready = {}
        xn_ready = {}

        def stage_a(s):
            u, hf = s // 2, s % 2
            b = slice(512 * hf, 512 * hf + 512)
            toks = []
            for n in range(2):
                h = 2 * u + n
                p = next_pq()
                pe.wait(wq_tok[h], [xn_ready[i] for i in range(4 * hf, 4 * hf + 4)])
                c = h % 3
                t = mm3(PQ[p][:, :], [(WQh[:, c, k * 128:(k + 1) * 128], WQl[:, c, k * 128:(k + 1) * 128],
                                       HTh[:, k, 1, b], HTl[:, k, 1, b]) for k in range(4)], s_mm)
                wq_free[c] = t
                dst = qb[:, s % 2, 0:1024].rearrange("p (b n t) -> p n b t", b=8, n=2)[:, n]
                toks.append(rope_out(p, t, dst, q_free[s % 2]))
            q_ready[s] = toks

        s_sc, s_tanh, s_msk, s_exp = sem("scores"), sem("tanh"), sem("masked"), sem("exp")
        s_sum, s_rec, s_nrm = sem("rowsum"), sem("rowrec"), sem("probs")
        s_tr, s_pt, s_av = sem("probsT"), sem("pT_sb"), sem("av")
        s_oh, s_ol, s_wo, s_x = sem("o_hi"), sem("o_lo"), sem("wo_ps"), sem("x_sum")
        ps_free = [None]
        pt_free = [None]
        pa_free = [None, None]
        o_free = [None, None]
        p_ready, pt_ready, o_ready = {}, {}, {}
        x_ready = {i: None for i in range(8)}
        rr_free = [None, None]

        def stage_b(s):
            u, hf = s // 2, s % 2
            j = u // 2
            pe.wait(ps_free[0], q_ready[s], k_ready[j][hf])
            for b in range(8):
                t = pe.run(lambda e, b=b: e.matmul(
                    PS[:, b * 64:(b + 1) * 64], qb[:, s % 2, b * 128:(b + 1) * 128],
                    kT[j % 2][:, 512 * hf + 64 * b:512 * hf + 64 * b + 64], start=True, stop=True),
                    s_sc if b == 7 else None)
            q_free[s % 2] = t
            if s % 4 >= 2:
                kt_free[j % 2] = t
            e2 = s % 2
            E = Eb[:, e2, :]
            E3 = E.rearrange("p (b t) -> p b t", b=8)
            act.wait(t, eb_free[e2])
            t1 = act.run(lambda e: e.activation(E, PS[:, :], ACT.Tanh, scale=ATT / CAP), s_tanh)
            ps_free[0] = t1
            dve.wait(t1, t_mb)
            t2 = dve.run(lambda e: e.scalar_tensor_tensor(
                E3, E3, many[:, 0:1], mbias[:, :].unsqueeze(1).broadcast_to([128, 8, 64]), ALU.mult, ALU.add), s_msk)
            act.wait(t2)
            t3 = act.run(lambda e: e.activation(E, E, ACT.Exp, scale=CAP), s_exp)
            dve.wait(t3, rr_free[e2])
            t4 = dve.run(lambda e: e.tensor_reduce(sm[:, e2, 0, :], E3, X, ALU.add), s_sum)
            dve.wait(t4)
            t5 = dve.run(lambda e: e.reciprocal(sm[:, e2, 1, :], sm[:, e2, 0, :]), s_rec)
            dve.wait(t5)
            t6 = dve.run(lambda e: e.tensor_tensor(
                E3, E3, sm[:, e2, 1, :].unsqueeze(2).broadcast_to([128, 8, 64]), ALU.mult), s_nrm)
            rr_free[e2] = t6
            p_ready[s] = t6

        def stage_c(s):
            e2 = s % 2
            pe.wait(pt_free[0], p_ready[s], t_ident)
            for c in range(4):
                t = pe.run(lambda e, c=c: e.transpose(PT[:, c * 128:(c + 1) * 128],
                                                      Eb[:, e2, c * 128:(c + 1) * 128], ident[:, :]),
                           s_tr if c == 3 else None)
            eb_free[e2] = t
            act.wait(t, ptb_free[e2])
            tp = act.run(lambda e: e.activation(pTb[:, e2, :], PT[:, :], ACT.Copy), s_pt)
            pt_free[0] = tp
            pt_ready[s] = tp

        def stage_d(s):
            u, hf = s // 2, s % 2
            j = u // 2
            e2 = s % 2
            V = V0[(j // 2) % 2]
            c0 = 128 * (j % 2)
            pe.wait(pt_ready[s])
            toks = [None, None]
            for b in range(8):
                r, c = b % 2, b // 2
                pe.wait(pa_free[r], v_ready[(j // 2, 4 * hf + c)])
                t = pe.run(lambda e, r=r, c=c: e.matmul(
                    PA[r][:, c * 128:c * 128 + 128],
                    V[64 * r:64 * r + 64, 4 * hf + c, c0:c0 + 128],
                    pTb[64 * r:64 * r + 64, e2, c * 128:(c + 1) * 128], start=True, stop=True),
                    s_av if c == 3 else None)
                toks[r] = t
            ptb_free[e2] = t
            if j % 2 == 1 and s % 4 == 3:
                v_free[(j // 2) % 2] = t
            ready = []
            for w in range(2):
                src = PA[w][:, :].rearrange("p (c n t) -> p c n t", c=4, n=2)
                dh, dl = (O[:, e2, :, :].rearrange("p n (c r t) -> p c r n t", c=4, r=2)[:, :, w] for O in (Oh, Ol))
                act.wait(toks[w], o_free[e2])
                th = act.run(lambda e, dh=dh, src=src: e.activation(dh, src, ACT.Copy), s_oh)
                dve.wait(th, o_free[e2])
                tl = dve.run(lambda e, dh=dh, dl=dl, src=src: e.tensor_tensor(dl, src, dh.bitcast(f32), ALU.subtract), s_ol)
                pa_free[w] = [th, tl]
                ready.append([th, tl])
            o_ready[s] = ready

        def stage_e(s):
            u, hf = s // 2, s % 2
            e2 = s % 2
            for c in range(4):
                i = 4 * hf + c
                p = next_po()
                pe.wait(o_ready[s], wo_tok[2 * u], wo_tok[2 * u + 1])
                t = mm3(PO[p][:, :], [(Oh[:, e2, n, c * 128:(c + 1) * 128], Ol[:, e2, n, c * 128:(c + 1) * 128],
                                       WOh[:, (2 * u + n) % 3, :], WOl[:, (2 * u + n) % 3, :]) for n in range(2)], s_wo)
                dve.wait(t, x_ready[i], xn_read[i])
                tx = dve.run(lambda e, i=i, p=p: e.tensor_tensor(xs[:, i, :], xs[:, i, :], PO[p][:, :], ALU.add), s_x)
                po_free[p] = tx
                x_ready[i] = tx
            o_free[e2] = t
            for n in range(2):
                wo_free[(2 * u + n) % 3] = t

        s_mb = sem("mask_bias")
        dve.wait(t_mask)
        t = dve.run(lambda e: e.tensor_copy(mbias[:, :], mask8), s_mb)
        dve.wait(t)
        t = dve.run(lambda e: e.tensor_reduce(many[:, 0:1], mbias[:, :], X, ALU.max), s_mb)
        dve.wait(t)
        t = dve.run(lambda e: e.tensor_scalar(mbias[:, :], mbias[:, :], -1.0, 1e4, ALU.add, ALU.mult), s_mb)
        dve.wait(t)
        t_mb = dve.run(lambda e: e.tensor_scalar(mbias[:, :], mbias[:, :], many[:, 0:1], None, ALU.mult), s_mb)
        dve.wait(t_mb)

        k_half(0, 0, wk_tok)
        t_ln = ln_prep(range(0, 4), t_x)
        for i in range(2):
            v_tile(0, i, wv_tok)
        load_wq(0)
        load_wq(1)
        ln_apply(range(0, 4), t_ln, None, xn_ready,
                 [lambda i=i: v_tile(0, i, wv_tok) for i in (2, 3)] + [lambda: k_half(0, 1, wk_tok)])
        t_ln = ln_prep(range(4, 8), t_x)
        stage_a(0)
        ln_apply(range(4, 8), t_ln, None, xn_ready, [lambda i=i: v_tile(0, i, wv_tok) for i in range(4, 8)])

        NS = 32
        for it in range(NS + 2):
            if it % 4 == 0 and it // 4 + 1 < 8:
                wk_tok = load_wk(it // 4 + 1)
            if it % 8 == 1 and it // 8 + 1 < 4:
                wv_tok = load_wv(it // 8 + 1)
            if it % 2 == 0 and it // 2 + 1 < 16:
                load_wq(it + 2)
            if it % 2 == 1 and it < NS:
                load_wo(it - 1)
            if 0 <= it - 1 < NS:
                stage_b(it - 1)
            if 0 <= it - 2 < NS:
                stage_d(it - 2)
            if 0 < it < NS:
                stage_a(it)
            if it % 2 == 1 and it + 2 < 32:
                load_wq(it + 2)
            if 0 <= it - 3 < NS:
                stage_e(it - 3)
            if it % 2 == 0 and 2 <= it <= NS:
                load_wo(it - 1)
            if it % 4 in (1, 2) and it // 4 + 1 < 8:
                k_half(it // 4 + 1, it % 4 - 1, wk_tok)
            if 3 <= it % 8 <= 6 and it // 8 + 1 < 4:
                for i in range(2):
                    v_tile(it // 8 + 1, 2 * (it % 8 - 3) + i, wv_tok)
            if 0 <= it - 1 < NS:
                stage_c(it - 1)

        sp.wait(q_free[0], q_free[1])
        t_aw = load(aw_sb, a["aw"].rearrange("p (k n) -> p k n", k=4), "aw")
        t_bc = load(bcat_sb, a["bcat"], "bcat")
        t_low = load(lowtri[:, :], a["lowtri"], "lowtri")
        s_mid, s_gt, s_ge = sem("ffn_mid"), sem("ffn_gate"), sem("ffn_exp")
        s_xf, s_mg, s_mT, s_mTs, s_dl = sem("ffn_xT"), sem("ffn_mg"), sem("ffn_mgT"), sem("ffn_mgTs"), sem("ffn_delta")

        def ffn_mid(hf, t):
            tiles = range(4 * hf, 4 * hf + 4)
            mid = mids[hf]
            for c, i in enumerate(tiles):
                s, tn = ln_xn(i, t)
                xn_read[i] = tn
                p, tt = ln_T(s, tn)
                f = c % 2
                act.wait(tt, ptb_free[f])
                tf = act.run(lambda e, p=p, f=f: e.activation(pTb[:, f, :], PQ[p][:, :], ACT.Copy), s_xf)
                pq_free[p] = tf
                pe.wait(tf, t_aw, ps_free[0], pt_free[0])
                for k in range(4):
                    tm = pe.run(lambda e, k=k, c=c, f=f: e.matmul(
                        mid[:, c, :], pTb[:, f, k * 128:(k + 1) * 128], aw_sb[:, k, :],
                        start=(k == 0), stop=(k == 3)), s_mid if k == 3 else None)
                ptb_free[f] = tm
            return tm

        def ffn_gates(hf, tm):
            mid = mids[hf]
            lg, g16, e16, gat, gs, midg = (small[hf][n] for n in ("lg", "g16", "e16", "gat", "gs", "midg"))
            dve.wait(tm, t_low)
            lj = lg.unsqueeze(2).broadcast_to([128, 4, 4, 4])
            le = lg.unsqueeze(3).broadcast_to([128, 4, 4, 4])
            G4 = g16.rearrange("p i (e j) -> p i e j", e=4)
            E4 = e16.rearrange("p i (e j) -> p i e j", e=4)
            low = lowtri[:, :].unsqueeze(1).broadcast_to([128, 4, 16])

            def chain(fs, s):
                for f in fs:
                    t = dve.run(f, s)
                    dve.wait(t)
                return t

            t = chain([
                lambda e: e.tensor_copy(lg, mid[:, :, 64:68]),
                lambda e: e.tensor_tensor(G4, lj, le, ALU.is_gt),
                lambda e: e.tensor_tensor(E4, lj, le, ALU.is_equal),
                lambda e: e.tensor_tensor(e16, e16, low, ALU.mult),
                lambda e: e.tensor_tensor(g16, g16, e16, ALU.add),
                lambda e: e.tensor_reduce(gat, G4, X, ALU.add),
                lambda e: e.tensor_scalar(gat, gat, 2.0, None, ALU.is_lt),
                lambda e: e.tensor_reduce(gs[:, 0, :], lg, X, ALU.max),
                lambda e: e.tensor_tensor(lg, lg, gs[:, 0, :].unsqueeze(2).broadcast_to([128, 4, 4]), ALU.subtract),
            ], s_gt)
            act.wait(t)
            t = act.run(lambda e: e.activation(lg, lg, ACT.Exp), s_ge)
            dve.wait(t)
            chain([
                lambda e: e.tensor_tensor(gat, gat, lg, ALU.mult),
                lambda e: e.tensor_reduce(gs[:, 1, :], gat, X, ALU.add),
                lambda e: e.reciprocal(gs[:, 2, :], gs[:, 1, :]),
                lambda e: e.scalar_tensor_tensor(
                    gat, gat, 4.0, gs[:, 2, :].unsqueeze(2).broadcast_to([128, 4, 4]), ALU.mult, ALU.mult),
            ], s_gt)
            for c in range(4):
                tg = dve.run(lambda e, c=c: e.tensor_tensor(
                    midg[:, c, :].rearrange("p (e r) -> p e r", e=4),
                    mid[:, c, 0:64].rearrange("p (e r) -> p e r", e=4),
                    gat[:, c, :].unsqueeze(2).broadcast_to([128, 4, 16]), ALU.mult), s_mg)
            return tg

        def ffn_delta(hf, tg):
            midg = small[hf]["midg"]
            f = hf
            p = next_pq()
            pe.wait(tg)
            for c in range(4):
                tt = pe.run(lambda e, c=c: e.transpose(PQ[p][0:64, c * 128:(c + 1) * 128], midg[:, c, :], ident[:, :]),
                            s_mT if c == 3 else None)
            act.wait(tt, ptb_free[f])
            tp = act.run(lambda e: e.activation(pTb[0:64, f, :], PQ[p][0:64, :], ACT.Copy), s_mTs)
            pq_free[p] = tp
            for c in range(4):
                i = 4 * hf + c
                p = next_po()
                pe.wait(tp, t_bc)
                td = pe.run(lambda e, c=c, p=p: e.matmul(PO[p][:, :], pTb[0:64, f, c * 128:(c + 1) * 128],
                                                         bcat_sb, start=True, stop=True), s_dl)
                dve.wait(td, x_ready[i], xn_read[i])
                tx = dve.run(lambda e, i=i, p=p: e.tensor_tensor(xs[:, i, :], xs[:, i, :], PO[p][:, :], ALU.add), s_x)
                po_free[p] = tx
                x_ready[i] = tx
            ptb_free[f] = td
            return td

        mids = [bank[:, 0:272].rearrange("p (i n) -> p i n", i=4) for bank in (PS, PT)]

        w1k_tok = {}

        def load_wk1(j):
            w1k_tok[j] = split_weight(a["wk1"][j], 128, 384, WKh[:, 0:384], WKl[:, 0:384], wk_free[0])

        wv1_home = [(WVh[:, 0:384], WVl[:, 0:384]), (WVh[:, 512:896], WVl[:, 512:896]),
                    (WOh[:, 2, 0:384], WOl[:, 2, 0:384]), (WOh[:, 0, 0:384], WOl[:, 0, 0:384])]
        wv1_tok = []

        def load_wv1(k):
            hi, lo = wv1_home[k]
            wv1_tok.extend(split_weight(a["wv1"][:, 384 * k:384 * k + 384], 128, 384, hi, lo,
                                        [wv_free[0], wo_free[2], wo_free[0]]))

        for k in range(3):
            load_wv1(k)
        load_wk1(0)
        wq1_tok, wo1_tok = {}, {}

        def load_wq1(j, m):
            wq1_tok[(j, m)] = split_weight(a["wq1"][3 * j + m], 128, 512, WQh[:, m, :], WQl[:, m, :], wq_free[m])

        wo1_home = [(WOh[:, c, :], WOl[:, c, :]) for c in range(3)] + [
            (WVh[:, c:c + 512], WVl[:, c:c + 512]) for c in (0, 512)]
        wo1_free = [None] * 5

        def load_wo1(j, m):
            c = (3 * j + m) % 5
            hi, lo = wo1_home[c]
            r0 = 384 * j + 128 * m
            wo1_tok[(j, m)] = split_weight(a["wo1"][r0:r0 + 128, :], 128, 512, hi, lo, wo1_free[c])

        for m in range(3):
            load_wq1(0, m)

        s_k1, s_v1 = sem("k1_sb"), sem("v1_sb")
        k1_free = [None, None]
        k1_ready = {}

        def k1_chunk(j, w, hf):
            p = next_pq()
            pe.wait(w1k_tok[j], ctx_ready)
            if w:
                pe.wait([xn_ready[i] for i in range(4 * hf, 4 * hf + 4)])
            b = slice(512 * hf, 512 * hf + 512)
            t = mm3(PQ[p][0:96, :], [(WKh[:, k * 96:(k + 1) * 96], WKl[:, k * 96:(k + 1) * 96],
                                      HTh[:, k, w, b], HTl[:, k, w, b]) for k in range(4)], s_mm)
            wk_free[0] = t
            src = PQ[p][0:96, :].rearrange("p (a r t) -> p a r t", a=4, r=2)
            dst = K1[j % 2].rearrange("p (a q t) -> p a q t", a=8, q=4)[:, 4 * hf:4 * hf + 4]
            dst = dst[:, :, 1:3, :] if w else dst[:, :, 0:4:3, :]
            act.wait(t, k1_free[j % 2])
            tk = act.run(lambda e: e.activation(dst, src, ACT.Copy), s_k1)
            pq_free[p] = tk
            k1_ready[(j, w, hf)] = tk

        v1_ready = {}

        def v1_tile(w, i):
            p = next_pq()
            pe.wait(wv1_tok, ctx_ready)
            if w:
                pe.wait(xn_ready[i])
            b = slice(128 * i, 128 * i + 128)
            t = mm3(PQ[p][:, 0:384], [(HTh[:, k, w, b], HTl[:, k, w, b],
                                       wv1_home[k][0], wv1_home[k][1]) for k in range(4)], s_mm)
            for c in range(5):
                wo1_free[c] = t
            act.wait(t)
            for r in range(2):
                at = 64 * (w ^ r)
                tv = act.run(lambda e, r=r, at=at: e.activation(V1[at:at + 64, 2 * i + r, :],
                                                                PQ[p][64 * r:64 * r + 64, 0:384], ACT.Copy), s_v1)
                v1_ready[(w, 2 * i + r)] = tv
            pq_free[p] = tv

        q1_ready = {}
        seam_done = [None]

        PACK = [[(0, 96, 0, 0), (96, 32, 1, 64)], [(0, 64, 1, 0), (64, 64, 2, 0)], [(0, 96, 3, 0), (96, 32, 2, 64)]]

        def stage_a1(g, m):
            j, hf = g // 2, g % 2
            b = slice(512 * hf, 512 * hf + 512)
            p = next_pq()
            pe.wait(wq1_tok[(j, m)], [xn_ready[i] for i in range(4 * hf, 4 * hf + 4)])
            t = mm3(PQ[p][:, :], [(WQh[:, m, k * 128:(k + 1) * 128], WQl[:, m, k * 128:(k + 1) * 128],
                                   HTh[:, k, 1, b], HTl[:, k, 1, b]) for k in range(4)], s_mm)
            wq_free[m] = t
            act.wait(t, q_free[g % 2], seam_done[0])
            for r0, n, h, d0 in PACK[m]:
                dst = qb[d0:d0 + n, g % 2, 1024 * (h // 2):1024 * (h // 2) + 1024].rearrange(
                    "p (b n t) -> p n b t", b=8, n=2)[:, h % 2]
                src = PQ[p][r0:r0 + n, :].rearrange("p (b t) -> p b t", b=8)
                tq = act.run(lambda e, dst=dst, src=src: e.activation(dst, src, ACT.Copy, scale=SC1), s_q1)
            pq_free[p] = tq
            q1_ready[g] = tq

        def stage_b1(s):
            j, qd, pr = s // 8, s % 8 // 2, s % 2
            g = 2 * j + qd // 2
            e2 = s % 2
            pe.wait(ps_free[0], q1_ready[g], k1_ready[(j, 0, qd // 2)], k1_ready[(j, 1, qd // 2)])
            for bb in range(4):
                b8, b = 4 * (qd % 2) + bb, 4 * qd + bb
                t = pe.run(lambda e, bb=bb, b8=b8, b=b: e.matmul(
                    PS[:, bb * 128:(bb + 1) * 128],
                    qb[0:96, g % 2, 1024 * pr + b8 * 128:1024 * pr + (b8 + 1) * 128],
                    K1[j % 2][:, b * 128:(b + 1) * 128], start=True, stop=True), s_sc if bb == 3 else None)
            q_free[g % 2] = t
            k1_free[j % 2] = t
            mx, rs = sm[:, e2, 0, 0:4], sm[:, e2, 0, 4:8]
            rr = sm[:, e2, 1, 0:4]
            E3 = Eb[:, e2, :].rearrange("p (b t) -> p b t", b=4)
            dve.wait(t, rr_free[e2])
            t1 = dve.run(lambda e: e.tensor_reduce(mx, PS[:, :].rearrange("p (b t) -> p b t", b=4), X, ALU.max,
                                                   negate=True), s_max)
            act.wait(t1, eb_free[e2])
            for bb in range(4):
                t2 = act.run(lambda e, bb=bb: e.activation(
                    Eb[:, e2, bb * 128:(bb + 1) * 128], PS[:, bb * 128:(bb + 1) * 128], ACT.Exp,
                    bias=mx[:, bb:bb + 1], accum_out=rs[:, bb:bb + 1]), s_exp)
            ps_free[0] = t2
            dve.wait(t2)
            t5 = dve.run(lambda e: e.reciprocal(rr, rs), s_rec)
            dve.wait(t5)
            t6 = dve.run(lambda e: e.tensor_tensor(E3, E3, rr.unsqueeze(2).broadcast_to([128, 4, 128]), ALU.mult), s_nrm)
            rr_free[e2] = t6
            p_ready[s] = t6

        Ohp, Olp = (O[:, :, :, :].rearrange("p s n t -> p s (n t)") for O in (Oh, Ol))
        o1_free = [None, None]
        o1_ready = {}

        def stage_d1(s):
            j, qd, pr = s // 8, s % 8 // 2, s % 2
            e2, os = s % 2, (s // 2) % 2
            pe.wait(pt_ready[s], pa_free[e2])
            for bb in range(4):
                b = 4 * qd + bb
                pe.wait(v1_ready[(0, b)], v1_ready[(1, b)])
                t = pe.run(lambda e, bb=bb, b=b: e.matmul(
                    PA[e2][0:96, bb * 128:(bb + 1) * 128], V1[:, b, 96 * j:96 * j + 96],
                    pTb[:, e2, bb * 128:(bb + 1) * 128], start=True, stop=True), s_av if bb == 3 else None)
            ptb_free[e2] = t
            act.wait(t, o1_free[os])
            moves = []
            for m in range(3):
                for r0, n, h, d0 in PACK[m]:
                    if h // 2 == pr:
                        src = PA[e2][d0:d0 + n, :].rearrange("p (b n t) -> p n b t", b=4, n=2)[:, h % 2]
                        dh, dl = (O[r0:r0 + n, os, 256 * m:256 * m + 256].rearrange("p (b t) -> p b t", b=4)
                                  for O in (Ohp, Olp))
                        th = act.run(lambda e, dh=dh, src=src: e.activation(dh, src, ACT.Copy), s_oh)
                        moves.append((src, dh, dl, th))
            dve.wait(o1_free[os], th)
            for src, dh, dl, _ in moves:
                tl = dve.run(lambda e, dh=dh, dl=dl, src=src: e.tensor_tensor(dl, src, dh.bitcast(f32), ALU.subtract), s_ol)
            pa_free[e2] = [th, tl]
            o1_ready[s] = [th, tl]

        def stage_e1(j, i):
            qd, c = i // 2, i % 2
            s = 8 * j + 2 * qd
            os = (s // 2) % 2
            p = next_po()
            pe.wait(o1_ready[s], o1_ready[s + 1], [wo1_tok[(j, m)] for m in range(3)])
            homes = [wo1_home[(3 * j + m) % 5] for m in range(3)]
            t = mm3(PO[p][:, :], [(Ohp[:, os, 256 * m + 128 * c:256 * m + 128 * c + 128],
                                   Olp[:, os, 256 * m + 128 * c:256 * m + 128 * c + 128],
                                   homes[m][0], homes[m][1]) for m in range(3)], s_wo)
            dve.wait(t, x_ready[i], xn_read[i])
            tx = dve.run(lambda e: e.tensor_tensor(xs[:, i, :], xs[:, i, :], PO[p][:, :], ALU.add), s_x)
            po_free[p] = tx
            x_ready[i] = tx
            o1_free[os] = t
            for m in range(3):
                wo1_free[(3 * j + m) % 5] = t

        s_q1, s_max = sem("q1_sb"), sem("rowmax")
        lo, hi = range(0, 4), range(4, 8)
        t_ln = ln_prep(lo, x_ready)
        stage_e(NS - 1)
        load_wv1(3)
        t_m0 = ffn_mid(0, t_ln)
        t_ln = ln_prep(hi, x_ready)
        t_g0 = ffn_gates(0, t_m0)
        k1_chunk(0, 0, 0)
        k1_chunk(0, 0, 1)
        load_wk1(1)
        t_m1 = ffn_mid(1, t_ln)
        ffn_delta(0, t_g0)
        t_g1 = ffn_gates(1, t_m1)
        t_ln = ln_prep(lo, x_ready)
        for i in range(4):
            v1_tile(0, i)
        xn_ready = {}
        seam_done[0] = ffn_delta(1, t_g1)
        ps_free[0] = t_g0
        pt_free[0] = t_g1
        ln_apply(lo, t_ln, None, xn_ready, [lambda i=i: v1_tile(0, i) for i in range(4, 8)])
        t_ln = ln_prep(hi, x_ready)
        for m in range(3):
            stage_a1(0, m)
        ln_apply(hi, t_ln, None, xn_ready,
                 [lambda c=c: k1_chunk(1, 0, c) for c in range(2)] + [lambda i=i: v1_tile(1, i) for i in range(2)])
        load_wk1(0)
        for i in range(2, 8):
            v1_tile(1, i)
        for hf in range(2):
            k1_chunk(0, 1, hf)
        load_wk1(1)

        weff_ready = []
        s_wc, s_bw, s_we, s_wa, s_wh, s_wl = (sem("w_col"), sem("b_scaled"), sem("weff_ps"), sem("weff_sum"),
                                              sem("weff_hi"), sem("weff_lo"))

        def ffn1_weights():
            sp.wait(k1_free[0])
            t_w = load(w1T, a["w1"].rearrange("p (k n) -> p k n", k=4), "w1")
            t_c = load(coef[:, 0:2], a["coef"], "coef")
            t_s = load(coef[:, 2:4], a["scl"], "scl")
            pieces = stage_load([(a["a1"][c], 128, 512) for c in range(2)] + [(a["bf1"][c], 128, 512) for c in range(2)])
            dve.wait(t_c, t_s)
            t = dve.run(lambda e: e.tensor_tensor(wcol[:, :], coef[:, 0:2], coef[:, 2:4], ALU.mult), s_wc)
            dve.wait(t)
            tb = []
            for c in range(2):
                i, tok = pieces[2 + c]
                dve.wait(tok)
                tb.append(dve.run(lambda e, i=i, c=c: e.tensor_scalar(stage[:, i, :], stage[:, i, :], wcol[:, c:c + 1],
                                                                      None, ALU.mult), s_bw))
            for m in range(4):
                p = next_pq()
                pe.wait(tb, pieces[0][1], pieces[1][1])
                for c in range(2):
                    ia, ib = pieces[c][0], pieces[2 + c][0]
                    t = pe.run(lambda e, ia=ia, ib=ib, c=c, m=m, p=p: e.matmul(
                        PQ[p][:, :], stage[:, ia, m * 128:(m + 1) * 128], stage[:, ib, :],
                        start=(c == 0), stop=(c == 1)), s_we if c == 1 else None)
                dve.wait(t, t_w)
                ta = dve.run(lambda e, m=m, p=p: e.tensor_tensor(w1T[:, m, :], w1T[:, m, :], PQ[p][:, :], ALU.add), s_wa)
                pq_free[p] = ta
                src = w1T[:, m, :]
                dh, dl = HTh[:, m, 0, 0:512], HTl[:, m, 0, 0:512]
                act.wait(ta, wk_free[0])
                th = act.run(lambda e, dh=dh, src=src: e.activation(dh, src, ACT.Copy), s_wh)
                dve.wait(ta, th, wk_free[0])
                tl = dve.run(lambda e, dh=dh, dl=dl, src=src: e.tensor_tensor(dl, src, dh.bitcast(f32), ALU.subtract), s_wl)
                weff_ready.extend([th, tl])
            for i, _ in pieces:
                stage_free[i] = t

        s_xb, s_y, s_out = sem("x_bias"), sem("y_ps"), sem("out")
        fin_ln, fin_ready, t_out = {}, {}, None

        def final(q):
            nonlocal t_out
            if q == 0:
                fin_ready["slot"] = stage_at[0] % 4
                (_, fin_ready["bias"]), = stage_load([(a["bias"], 128, 512)])
            biasb = stage[:, fin_ready["slot"], :]
            if 2 <= q < 6:
                for i in (2 * q - 4, 2 * q - 3):
                    p = next_po()
                    pe.wait(fin_ready[i], weff_ready)
                    b = slice(128 * i, 128 * i + 128)
                    t = mm3(PO[p][:, :], [(HTh[:, k, 1, b], HTl[:, k, 1, b], HTh[:, k, 0, 0:512], HTl[:, k, 0, 0:512])
                                          for k in range(4)], s_y)
                    dve.wait(t, fin_ready[("b", i)])
                    ty = dve.run(lambda e, i=i, p=p: e.tensor_tensor(xs[:, i, :], xs[:, i, :], PO[p][:, :], ALU.add), s_x)
                    po_free[p] = ty
                    sp.wait(ty)
                    t_out = sp.run(lambda e, i=i: e.dma_start(out[i * 128:(i + 1) * 128, :], xs[:, i, :]), s_out, 16)
            if 1 <= q < 5:
                tiles = (2 * q - 2, 2 * q - 1)
                ln_apply(tiles, fin_ln[q - 1], [q_free[0], q_free[1]], fin_ready)
                for i in tiles:
                    pool.wait(fin_ready["bias"], xn_read[i], x_ready[i])
                    fin_ready[("b", i)] = pool.run(
                        lambda e, i=i: e.tensor_tensor(xs[:, i, :], xs[:, i, :], biasb, ALU.add), s_xb)
            if q < 4:
                fin_ln[q] = ln_prep((2 * q, 2 * q + 1), x_ready)

        N1 = 32
        k1_plan = {4: (1, 1, 0), 7: (1, 1, 1)}
        for j in (2, 3):
            k1_plan.update({8 * j - 8: (j, 0, 0), 8 * j - 6: (j, 1, 0), 8 * j - 4: (j, 0, 1), 8 * j - 2: (j, 1, 1)})
        for it in range(N1 + 10):
            if it < N1 and it % 8 == 0:
                load_wo1(it // 8, 0)
                load_wo1(it // 8, 1)
                if 2 <= it // 8 + 1 < 4:
                    load_wk1(it // 8 + 1)
            if 0 <= it - 1 < N1:
                stage_b1(it - 1)
            if 0 <= it - 2 < N1:
                stage_d1(it - 2)
            g, m = (it + 3) // 4, (it + 3) % 4
            if 1 <= g < 8 and m < 3:
                stage_a1(g, m)
                if g % 2 == 1 and g // 2 + 1 < 4:
                    load_wq1(g // 2 + 1, m)
            if it in k1_plan:
                k1_chunk(*k1_plan[it])
            if 0 <= it - 4 < N1:
                stage_e1((it - 4) // 8, (it - 4) % 8)
            if it % 8 == 3 and it < N1:
                load_wo1(it // 8, 2)
            if 0 <= it - 1 < N1:
                stage_c(it - 1)
            if it == 28:
                ffn1_weights()
            if it >= 29 and it % 2 == 1:
                final((it - 29) // 2)

        sp.wait(t_out)

        block = ctx.enter_context(nc.Block())

        @block.sync
        def _(e):
            sp.emit(e)

        @block.scalar
        def _(e):
            act.emit(e)

        @block.gpsimd
        def _(e):
            pool.emit(e)

        @block.vector
        def _(e):
            dve.emit(e)

        @block.tensor
        def _(e):
            pe.emit(e)


def kernel(**inputs):
    import numpy as np
    import concourse.bacc as bacc
    from concourse.bass_utils import run_bass_kernel_spmd as run

    g = {k: np.asarray(v) for k, v in inputs.items()}
    half = np.float32(1.0) / np.float32(10000.0) ** (np.arange(0, 128, 2, dtype=np.float32) / np.float32(128))
    phase = np.arange(64, dtype=np.float32)[None, :] * half.astype(np.float32)[:, None]
    cos, sin = np.cos(phase), np.sin(phase)
    rope = np.concatenate([np.concatenate([cos, cos], 0), np.concatenate([sin, -sin], 0)], 1)
    low = np.array([[1.0 if j < e else 0.0 for j in range(4)] for e in range(4)], np.float32).reshape(1, 16)
    pk = lambda w: w.reshape(4, 128, -1).transpose(1, 0, 2)
    heads = lambda w, n: w.reshape(4, 128, n, -1).transpose(2, 1, 0, 3).reshape(n, 128, -1)
    rows = np.concatenate([96 * h + np.arange(d, d + n) for h, d, n in (
        (0, 0, 96), (1, 64, 32), (1, 0, 64), (2, 0, 64), (3, 0, 96), (2, 64, 32))])
    packed = lambda w: w.reshape(4, 384, 512)[:, rows].reshape(1536, 512)
    a = {
        "x": g["x"].reshape(1024, 512),
        "ctxT": g["ctx_4096"].reshape(1024, 512).T,
        "mask": np.concatenate([g["mask_1x1xSxS2_bk0"].reshape(64, 64)] * 2, 0).view(np.int32),
        "rope": rope.astype(np.float32),
        "ident": np.eye(128, dtype=np.float32),
        "lowtri": np.broadcast_to(low, (128, 16)),
        "wq0": heads(g["L0_xattn_Wq"], 32),
        "wk0": heads(g["L0_xattn_Wk"], 8),
        "wv0": heads(g["L0_xattn_Wv"], 4),
        "wo0": g["L0_xattn_Wo"],
        "aw": pk(np.concatenate([g["L0_ffn_A"].reshape(64, 512), g["L0_ffn_Wr"]], 0).T).reshape(128, 272),
        "bcat": g["L0_ffn_B"].transpose(0, 2, 1).reshape(64, 512),
        "wq1": heads(packed(g["L1_xattn_Wq"]).T, 12),
        "wk1": heads(g["L1_xattn_Wk"].T, 4),
        "wv1": pk(g["L1_xattn_Wv"].T).reshape(128, 1536),
        "wo1": packed(g["L1_xattn_Wo"].T),
        "w1": pk(g["L1_ffn_W"].T).reshape(128, 2048),
        "a1": g["L1_ffn_A"].reshape(2, 128, 512),
        "bf1": g["L1_ffn_Bf"].transpose(0, 2, 1).reshape(2, 128, 512),
        "coef": np.repeat(g["L1_ffn_coeffs"], 16).reshape(2, 128).T,
        "scl": np.repeat(g["L1_ffn_scales"], 16).reshape(2, 128).T,
        "bias": np.broadcast_to(g["L1_ffn_bias"][None, :], (128, 512)),
    }
    nc = bacc.Bacc("TRN2", target_bir_lowering=False, num_devices=1)
    arrays, aps = {}, {}
    for name in INS:
        v = np.ascontiguousarray(a[name])
        arrays["in_" + name] = v
        aps[name] = nc.dram_tensor("in_" + name, v.shape, mybir.dt.from_np(v.dtype), kind="ExternalInput").ap()
    out = nc.dram_tensor("out_0", (1024, 512), mybir.dt.float32, kind="ExternalOutput").ap()
    program(nc, aps, out)
    r = run(nc, [arrays], core_ids=[0])
    return np.asarray(r.results[0]["out_0"]).reshape(16, 64, 512)
```

```python
import concourse.bass as bass
from concourse import mybir
from contextlib import ExitStack

INS = ["x", "ctxT", "mask", "rope", "ident", "lowtri", "wq0", "wk0", "wv0", "wo0", "aw", "bcat",
       "wq1", "wk1", "wv1", "wo1", "w1", "a1", "bf1", "coef", "scl", "bias"]


class Lane:

    def __init__(self):
        self.items = []
        self.passed = {}

    def wait(self, *tokens):
        for tok in tokens:
            if tok is None:
                continue
            if isinstance(tok, list):
                self.wait(*tok)
                continue
            sem, value = tok
            if self.passed.get(sem.name, 0) < value:
                self.passed[sem.name] = value
                self.items.append((None, sem, value))

    def run(self, fn, sem=None, n=1):
        self.items.append((fn, sem, n))
        if sem is not None:
            sem.count += n
            return (sem, sem.count)

    def emit(self, eng):
        for fn, sem, n in self.items:
            if fn is None:
                eng.wait_ge(sem.handle, n)
            else:
                ins = fn(eng)
                if sem is not None:
                    ins.then_inc(sem.handle, n)


class Sem:
    def __init__(self, handle, name):
        self.handle, self.name, self.count = handle, name, 0


def program(nc, a, out):
    f32 = mybir.dt.float32
    f32r = mybir.dt.float32r
    i32 = mybir.dt.int32
    u8 = mybir.dt.uint8
    ALU = mybir.AluOpType
    ACT = mybir.ActivationFunctionType
    X = mybir.AxisListType.X
    ATT = 0.08838834764831845
    CAP = 30.0
    EPS = 1e-5
    SC1 = 1.0 / 96.0 ** 0.5

    with ExitStack() as ctx:
        def sb(name, shape, dt=f32):
            return ctx.enter_context(nc.sbuf_tensor(name, shape, dt))

        def sem(name):
            return Sem(ctx.enter_context(nc.semaphore(name)), name)

        xs = sb("xs", [128, 8, 512])
        xTh = sb("xTh", [128, 4, 1024], f32r)
        xTl = sb("xTl", [128, 4, 1024], f32r)
        arena = sb("arena", [128, 10240])
        kT = [arena[:, s * 1024:(s + 1) * 1024] for s in range(2)]
        V0 = [arena[:, 2048 + s * 2048:2048 + (s + 1) * 2048].rearrange("p (i n) -> p i n", i=8) for s in range(2)]
        rtmp = [arena[:, 6144 + s * 512:6144 + (s + 1) * 512] for s in range(2)]
        K1 = [arena[0:96, j * 2048:(j + 1) * 2048] for j in range(4)]
        w1T = arena[:, 8192:10240].rearrange("p (k n) -> p k n", k=4)
        ab_sb = arena[:, 0:2048].rearrange("p (c n) -> p c n", c=4)
        qb = sb("qb", [128, 2, 2048])
        aw_sb = qb[:, 0, 0:272].rearrange("p (k n) -> p k n", k=4)
        bcat_sb = qb[0:64, 0, 512:1024]
        Eb = sb("Eb", [128, 2, 512])
        pTb = sb("pTb", [128, 2, 512])
        Oh = sb("Oh", [128, 2, 2, 512], f32r)
        Ol = sb("Ol", [128, 2, 2, 512], f32r)
        WQh = sb("WQh", [128, 3, 512], f32r)
        WQl = sb("WQl", [128, 3, 512], f32r)
        WOh = sb("WOh", [128, 3, 512], f32r)
        WOl = sb("WOl", [128, 3, 512], f32r)
        WKh = sb("WKh", [128, 512], f32r)
        WKl = sb("WKl", [128, 512], f32r)
        WVh = sb("WVh", [128, 1024], f32r)
        WVl = sb("WVl", [128, 1024], f32r)
        stage = sb("stage", [128, 4, 512])
        rope = sb("rope", [128, 2, 64])
        ident = sb("ident_sb", [128, 128])
        mask32 = sb("mask32", [128, 16], i32)
        mask8 = mask32[:, :].bitcast(u8)
        mbias = sb("mbias", [128, 64])
        many = sb("many", [128, 1])
        lowtri = sb("lowtri_sb", [128, 16])
        coef = sb("coef_sb", [128, 4])
        wcol = sb("wcol", [128, 2])
        st6 = sb("st6", [128, 8, 6])
        mv = sb("mv", [128, 8, 2])
        lnb = sb("lnb", [128, 5, 8])
        sm = sb("sm", [128, 2, 2, 8])
        small = []
        for h in range(2):
            at = 512 * h
            small.append({})
            for n, r, c in (("lg", 4, 4), ("g16", 4, 16), ("e16", 4, 16), ("gat", 4, 4), ("gs", 3, 4), ("midg", 4, 64)):
                small[h][n] = qb[:, 1, at:at + r * c].rearrange("p (r c) -> p r c", r=r)
                at += r * c
        with nc.sbuf_tensor("cTh", [128, 4, 1024], f32r) as cTh, nc.sbuf_tensor("cTl", [128, 4, 1024], f32r) as cTl:
            pass
        V1 = [sb(f"V1{r}", [128, 4, 1024]) for r in range(2)]
        HTh, HTl = (cTh, xTh), (cTl, xTl)
        PB = [ctx.enter_context(nc.psum_tensor(f"PB{i}", [128, 512], f32)) for i in range(8)]
        PS, PT, PA = PB[2], PB[3], PB[4:6]

        pe, act, dve, pool, sp = Lane(), Lane(), Lane(), Lane(), Lane()

        def load(dst, src, name):
            s = sem("ld_" + name)
            return sp.run(lambda e: e.dma_start(dst, src), s, 16)

        s_stage = [sem(f"ld_stage{i}") for i in range(4)]
        stage_free = [None] * 4
        stage_at = [0]

        def stage_load(pieces):
            got = []
            for src, rows, cols in pieces:
                i = stage_at[0] % 4
                stage_at[0] += 1
                sp.wait(stage_free[i])
                dst = stage[0:rows, i, 0:cols]
                tok = sp.run(lambda e, dst=dst, src=src: e.dma_start(dst, src), s_stage[i], 16)
                got.append((i, tok))
            return got

        s_whi, s_wlo = sem("w_hi"), sem("w_lo")

        def split_weight(src, rows, cols, hi, lo, free, pool_too=False):
            (i, tok), = stage_load([(src, rows, cols)])
            piece = stage[0:rows, i, 0:cols]
            act.wait(tok, free)
            th = act.run(lambda e: e.activation(hi, piece, ACT.Copy), s_whi)
            pool.wait(tok, th, free)
            tl = pool.run(lambda e: e.tensor_tensor(lo, piece, hi.bitcast(f32), ALU.subtract), s_wlo)
            stage_free[i] = tl
            return [tl]

        bank_free = [None] * 8
        held = []
        ring = [0, 1, 6, 7, 2, 3, 4, 5]

        def next_bank():
            i = ring.pop(0)
            ring.append(i)
            assert i not in held
            pe.wait(bank_free[i])
            return i

        s_mm = sem("mm_proj")

        def mm3(dst, pairs, s):
            steps = []
            for Ah, Al, Bh, Bl, *tok in pairs:
                steps += [(Ah, Bh, tok), (Ah, Bl, None), (Al, Bh, None)]
            for n, (A, B, tok) in enumerate(steps):
                last = n == len(steps) - 1
                pe.wait(tok)
                tok = pe.run(lambda e, A=A, B=B, n=n, last=last: e.matmul(dst, A, B, start=(n == 0), stop=last),
                             s if last else None)
            return tok

        cst = [[arena[:, 2048 + h * 2048 + 512 * k:2048 + h * 2048 + 512 * k + 512] for h in range(2)] for k in range(4)]
        wk_free = [None]
        wv_free = [None]

        def load_wk(j):
            return split_weight(a["wk0"][j], 128, 512, WKh[:, :], WKl[:, :], wk_free[0])

        def load_wv(p):
            toks = []
            for c in range(2):
                cols = slice(512 * c, 512 * c + 512)
                toks += split_weight(a["wv0"][p][:, cols], 128, 512, WVh[:, cols], WVl[:, cols], wv_free[0])
            return toks

        s_ctx, s_ctl = sem("ctx_hi"), sem("ctx_lo")
        ctx_half = [[], []]
        ctx_piece = {}

        def load_ctx(h):
            cols = slice(512 * h, 512 * h + 512)
            got = [load(cst[k][h], a["ctxT"][k * 128:(k + 1) * 128, cols], f"ctx{k}{h}") for k in range(4)]
            for k in range(4):
                src = cst[k][h]
                act.wait(got[k])
                th = act.run(lambda e, k=k, src=src: e.activation(HTh[0][:, k, cols], src, ACT.Copy), s_ctx)
                dve.wait(got[k], th)
                tl = dve.run(lambda e, k=k, src=src: e.tensor_tensor(
                    HTl[0][:, k, cols], src, HTh[0][:, k, cols].bitcast(f32), ALU.subtract), s_ctl)
                ctx_half[h] = [tl]
                ctx_piece[(h, k)] = tl

        wk_tok = load_wk(0)
        load_ctx(0)
        t_x = [load(xs[:, i, :], a["x"][i * 128:(i + 1) * 128, :], f"x{i}") for i in range(4)]
        wv_tok = load_wv(0)
        t_ident = load(ident[:, :], a["ident"], "ident")
        t_rope = load(rope[:, :, :], a["rope"].rearrange("p (a n) -> p a n", a=2), "rope")
        ctx_ready = ctx_half

        s_st, s_ln, s_xn, s_xt = sem("ln_stats"), sem("ln_rstd"), sem("ln_xn"), sem("ln_T")
        s_xh, s_xl = sem("ln_hi"), sem("ln_lo")
        eb_free = [None, None]
        ptb_free = [None, None]

        def ln_stats(i, x_tok):
            dve.wait(x_tok)
            t = dve.run(lambda e: e.bn_stats(st6[:, i, :], xs[:, i, :]), s_st)
            dve.wait(t)
            return dve.run(lambda e: e.bn_aggr(mv[:, i, :], st6[:, i, :]), s_st)

        def ln_rstd(i0, n, tok, free):
            r = slice(i0, i0 + n)
            v, y, b, c, nm = (lnb[:, m, r] for m in range(5))
            dve.wait(tok, free)
            steps = [
                lambda e: e.tensor_scalar(v, mv[:, r, 1], EPS, None, ALU.add),
                lambda e: e.tensor_scalar(y.bitcast(i32), v.bitcast(i32), -0.5, 1597463007.0, ALU.mult, ALU.add),
            ]
            for _ in range(3):
                steps += [
                    lambda e: e.scalar_tensor_tensor(b, y, -0.5, y, ALU.mult, ALU.mult),
                    lambda e: e.tensor_tensor(c, b, v, ALU.mult),
                    lambda e: e.scalar_tensor_tensor(y, c, 1.5, y, ALU.add, ALU.mult),
                ]
            steps.append(lambda e: e.scalar_tensor_tensor(nm, mv[:, r, 0], -1.0, y, ALU.mult, ALU.mult))
            for f in steps:
                t = dve.run(f, s_ln)
                dve.wait(t)
            return t

        ln_at = [0]

        def ln_xn(i, tok):
            s = ln_at[0] % 2
            ln_at[0] += 1
            act.wait(tok, eb_free[s])
            return s, act.run(lambda e: e.activation(Eb[:, s, :], xs[:, i, :], ACT.Identity,
                                                     bias=lnb[:, 4, i:i + 1], scale=lnb[:, 1, i:i + 1]), s_xn)

        def ln_T(s, tok):
            p = next_bank()
            pe.wait(tok, t_ident)
            for k in range(4):
                t = pe.run(lambda e, k=k: e.transpose(PB[p][:, k * 128:(k + 1) * 128],
                                                      Eb[:, s, k * 128:(k + 1) * 128], ident[:, :]),
                           s_xt if k == 3 else None)
            eb_free[s] = t
            return p, t

        def ln_split(i, p, tok, free):
            src = PB[p][:, :].rearrange("p (k t) -> p k t", k=4)
            cols = slice(128 * i, 128 * i + 128)
            act.wait(tok, free)
            th = act.run(lambda e: e.activation(HTh[1][:, :, cols], src, ACT.Copy), s_xh)
            dve.wait(th, free)
            tl = dve.run(lambda e: e.tensor_tensor(
                HTl[1][:, :, cols], src, HTh[1][:, :, cols].bitcast(f32), ALU.subtract), s_xl)
            bank_free[p] = tl
            return tl

        xn_read = [None] * 8

        def ln_prep(tiles, x_tok, free=None, done=()):
            st = list(done) + [ln_stats(i, x_tok[i]) for i in tiles[len(done):]]
            return ln_rstd(tiles[0], len(tiles), st, free)

        def ln_apply(tiles, tok, free, ready, filler=(), first=()):
            tiles, filler = list(tiles), list(filler)
            xn = {}

            def start(i):
                xn[i] = ln_xn(i, tok)
                xn_read[i] = xn[i][1]

            for i in tiles[:2]:
                start(i)
            for f in first:
                f()
            for n, i in enumerate(tiles):
                p, tt = ln_T(*xn[i])
                if n + 2 < len(tiles):
                    start(tiles[n + 2])
                ready[i] = ln_split(i, p, tt, free)
                f = filler.pop(0) if filler else None
                if f:
                    f()
            for f in filler:
                f()

        s_ra, s_rb, s_rc, s_rq = sem("rope_cos"), sem("rope_sin"), sem("rope_sin2"), sem("rope_sum")
        rtmp_free = [None, None]
        rt_at = [0]

        def rope_out(p, tok, dst, free):
            r = rt_at[0] % 2
            rt_at[0] += 1
            src = PB[p][:, :].rearrange("p (b t) -> p b t", b=8)
            tmp = rtmp[r].rearrange("p (b t) -> p b t", b=8)
            cos = rope[:, 0:1, :].broadcast_to([128, 8, 64])
            dve.wait(tok, free, t_rope, rtmp_free[r])
            ta = dve.run(lambda e: e.tensor_tensor(dst, src, cos, ALU.mult), s_ra)
            tb = dve.run(lambda e: e.tensor_tensor(
                tmp[0:64], src[64:128], rope[64:128, 1:2, :].broadcast_to([64, 8, 64]), ALU.mult), s_rb)
            tc = dve.run(lambda e: e.tensor_tensor(
                tmp[64:128], src[0:64], rope[0:64, 1:2, :].broadcast_to([64, 8, 64]), ALU.mult), s_rc)
            bank_free[p] = tc
            pool.wait(ta, tb, tc)
            tq = pool.run(lambda e: e.tensor_tensor(dst, dst, tmp, ALU.add), s_rq)
            rtmp_free[r] = tq
            return tq

        kt_free = [None, None]
        k_ready = {}

        def k_half(j, hf, tok):
            p = next_bank()
            pe.wait(tok)
            b = slice(512 * hf, 512 * hf + 512)
            t = mm3(PB[p][:, :], [(WKh[:, k * 128:(k + 1) * 128], WKl[:, k * 128:(k + 1) * 128],
                                   HTh[0][:, k, b], HTl[0][:, k, b], ctx_piece[(hf, k)]) for k in range(4)], s_mm)
            wk_free[0] = t
            dst = kT[j % 2][:, 512 * hf:512 * hf + 512].rearrange("p (b t) -> p b t", b=8)
            k_ready.setdefault(j, []).append(rope_out(p, t, dst, kt_free[j % 2]))

        v_free = [ctx_ready, ctx_ready]
        v_ready = {}
        s_v = sem("v_sb")

        def v_tile(pr, i, tok, later=None):
            p = next_bank()
            pe.wait(tok, ctx_half[i // 4])
            b = slice(128 * i, 128 * i + 128)
            t = mm3(PB[p][:, 0:256], [(HTh[0][:, k, b], HTl[0][:, k, b],
                                       WVh[:, k * 256:(k + 1) * 256], WVl[:, k * 256:(k + 1) * 256])
                                      for k in range(4)], s_mm)
            wv_free[0] = t

            def move():
                act.wait(t, v_free[pr % 2])
                tv = act.run(lambda e: e.activation(V0[pr % 2][:, i, :], PB[p][:, 0:256], ACT.Copy), s_v)
                bank_free[p] = tv
                v_ready[(pr, i)] = tv

            if later is None:
                move()
            else:
                later.append(move)

        wq_free = [None] * 3
        wo_free = [None] * 3
        wq_tok, wo_tok = {}, {}

        def load_wq(h):
            wq_tok[h] = split_weight(a["wq0"][h], 128, 512, WQh[:, h % 3, :], WQl[:, h % 3, :], wq_free[h % 3])

        def load_wo(h):
            wo_tok[h] = split_weight(a["wo0"][h * 128:(h + 1) * 128, :], 128, 512, WOh[:, h % 3, :],
                                     WOl[:, h % 3, :], wo_free[h % 3])

        q_free = [None, None]
        q_ready = {}
        xn_ready = {}

        def stage_a(s):
            u, hf = s // 2, s % 2
            b = slice(512 * hf, 512 * hf + 512)
            toks = []
            for n in range(2):
                h = 2 * u + n
                p = next_bank()
                pe.wait(wq_tok[h], xn_ready[4 * hf + 3])
                c = h % 3
                t = mm3(PB[p][:, :], [(WQh[:, c, k * 128:(k + 1) * 128], WQl[:, c, k * 128:(k + 1) * 128],
                                       HTh[1][:, k, b], HTl[1][:, k, b]) for k in range(4)], s_mm)
                wq_free[c] = t
                dst = qb[:, s % 2, 0:1024].rearrange("p (b n t) -> p n b t", b=8, n=2)[:, n]
                toks.append(rope_out(p, t, dst, q_free[s % 2]))
            q_ready[s] = toks[-1]

        s_sc, s_tanh, s_msk, s_exp = sem("scores"), sem("tanh"), sem("masked"), sem("exp")
        s_sum, s_rec, s_nrm = sem("rowsum"), sem("rowrec"), sem("probs")
        s_tr, s_pt, s_av = sem("probsT"), sem("pT_sb"), sem("av")
        s_oh, s_ol, s_wo, s_x = sem("o_hi"), sem("o_lo"), sem("wo_ps"), sem("x_sum")
        o_free = [None, None]
        p_ready, pt_ready, o_ready = {}, {}, {}
        x_ready = {i: None for i in range(8)}
        rr_free = [None, None]

        def stage_b(s):
            u, hf = s // 2, s % 2
            j = u // 2
            pe.wait(bank_free[2], q_ready[s], k_ready[j][hf])
            for b in range(8):
                t = pe.run(lambda e, b=b: e.matmul(
                    PS[:, b * 64:(b + 1) * 64], qb[:, s % 2, b * 128:(b + 1) * 128],
                    kT[j % 2][:, 512 * hf + 64 * b:512 * hf + 64 * b + 64], start=True, stop=True),
                    s_sc if b == 7 else None)
            q_free[s % 2] = t
            if s % 4 >= 2:
                kt_free[j % 2] = t
            e2 = s % 2
            E = Eb[:, e2, :]
            E3 = E.rearrange("p (b t) -> p b t", b=8)
            act.wait(t, eb_free[e2])
            t1 = act.run(lambda e: e.activation(E, PS[:, :], ACT.Tanh, scale=ATT / CAP), s_tanh)
            bank_free[2] = t1
            dve.wait(t1, t_mb)
            t2 = dve.run(lambda e: e.scalar_tensor_tensor(
                E3, E3, many[:, 0:1], mbias[:, :].unsqueeze(1).broadcast_to([128, 8, 64]), ALU.mult, ALU.add), s_msk)
            act.wait(t2)
            t3 = act.run(lambda e: e.activation(E, E, ACT.Exp, scale=CAP), s_exp)
            dve.wait(t3, rr_free[e2])
            t4 = dve.run(lambda e: e.tensor_reduce(sm[:, e2, 0, :], E3, X, ALU.add), s_sum)
            dve.wait(t4)
            t5 = dve.run(lambda e: e.reciprocal(sm[:, e2, 1, :], sm[:, e2, 0, :]), s_rec)
            dve.wait(t5)
            t6 = dve.run(lambda e: e.tensor_tensor(
                E3, E3, sm[:, e2, 1, :].unsqueeze(2).broadcast_to([128, 8, 64]), ALU.mult), s_nrm)
            rr_free[e2] = t6
            p_ready[s] = t6

        def stage_c(s):
            e2 = s % 2
            pe.wait(bank_free[3], p_ready[s], t_ident)
            for c in range(4):
                t = pe.run(lambda e, c=c: e.transpose(PT[:, c * 128:(c + 1) * 128],
                                                      Eb[:, e2, c * 128:(c + 1) * 128], ident[:, :]),
                           s_tr if c == 3 else None)
            eb_free[e2] = t
            act.wait(t, ptb_free[e2])
            tp = act.run(lambda e: e.activation(pTb[:, e2, :], PT[:, :], ACT.Copy), s_pt)
            bank_free[3] = tp
            pt_ready[s] = tp

        def stage_d(s):
            u, hf = s // 2, s % 2
            j = u // 2
            e2 = s % 2
            V = V0[(j // 2) % 2]
            c0 = 128 * (j % 2)
            pe.wait(pt_ready[s])
            toks = [None, None]
            for b in range(8):
                r, c = b % 2, b // 2
                pe.wait(bank_free[4 + r], v_ready[(j // 2, 4 * hf + c)])
                t = pe.run(lambda e, r=r, c=c: e.matmul(
                    PA[r][:, c * 128:c * 128 + 128],
                    V[64 * r:64 * r + 64, 4 * hf + c, c0:c0 + 128],
                    pTb[64 * r:64 * r + 64, e2, c * 128:(c + 1) * 128], start=True, stop=True),
                    s_av if c == 3 else None)
                toks[r] = t
            ptb_free[e2] = t
            if j % 2 == 1 and s % 4 == 3:
                v_free[(j // 2) % 2] = t
            ready = []
            for w in range(2):
                src = PA[w][:, :].rearrange("p (c n t) -> p c n t", c=4, n=2)
                dh, dl = (O[:, e2, :, :].rearrange("p n (c r t) -> p c r n t", c=4, r=2)[:, :, w] for O in (Oh, Ol))
                act.wait(toks[w], o_free[e2])
                th = act.run(lambda e, dh=dh, src=src: e.activation(dh, src, ACT.Copy), s_oh)
                dve.wait(th, o_free[e2])
                tl = dve.run(lambda e, dh=dh, dl=dl, src=src: e.tensor_tensor(dl, src, dh.bitcast(f32), ALU.subtract), s_ol)
                bank_free[4 + w] = tl
                ready.append(tl)
            o_ready[s] = ready[-1]

        def stage_e(s):
            u, hf = s // 2, s % 2
            e2 = s % 2
            for c in range(4):
                i = 4 * hf + c
                p = next_bank()
                pe.wait(o_ready[s], wo_tok[2 * u + 1])
                t = mm3(PB[p][:, :], [(Oh[:, e2, n, c * 128:(c + 1) * 128], Ol[:, e2, n, c * 128:(c + 1) * 128],
                                       WOh[:, (2 * u + n) % 3, :], WOl[:, (2 * u + n) % 3, :]) for n in range(2)], s_wo)
                dve.wait(t, x_ready[i], xn_read[i])
                tx = dve.run(lambda e, i=i, p=p: e.tensor_tensor(xs[:, i, :], xs[:, i, :], PB[p][:, :], ALU.add), s_x)
                bank_free[p] = tx
                x_ready[i] = tx
            o_free[e2] = t
            for n in range(2):
                wo_free[(2 * u + n) % 3] = t

        t_ln = ln_prep(range(0, 4), t_x)
        load_wq(0)
        load_wq(1)
        k_half(0, 0, wk_tok)
        later = []
        v_now = [lambda i=i: v_tile(0, i, wv_tok, later) for i in range(4)]
        ln_apply(range(0, 4), t_ln, None, xn_ready, [None] + v_now[3:], v_now[:3])
        for move in later:
            move()
        load_ctx(1)
        t_x += [load(xs[:, i, :], a["x"][i * 128:(i + 1) * 128, :], f"x{i}") for i in range(4, 8)]
        t_mask = load(mask32[:, :], a["mask"], "mask")
        t_ln = ln_prep(range(4, 8), t_x)
        stage_a(0)

        s_mb = sem("mask_bias")
        dve.wait(t_mask)
        t = dve.run(lambda e: e.tensor_copy(mbias[:, :], mask8), s_mb)
        dve.wait(t)
        t = dve.run(lambda e: e.tensor_reduce(many[:, 0:1], mbias[:, :], X, ALU.max), s_mb)
        dve.wait(t)
        t = dve.run(lambda e: e.tensor_scalar(mbias[:, :], mbias[:, :], -1.0, 1e4, ALU.add, ALU.mult), s_mb)
        dve.wait(t)
        t_mb = dve.run(lambda e: e.tensor_scalar(mbias[:, :], mbias[:, :], many[:, 0:1], None, ALU.mult), s_mb)
        k_half(0, 1, wk_tok)
        v_now = [lambda i=i: v_tile(0, i, wv_tok) for i in range(4, 8)]
        ln_apply(range(4, 8), t_ln, None, xn_ready, v_now[1:], v_now[:1])

        ffn_in = {}

        def load_ffn():
            sp.wait(q_free[0])
            ffn_in["aw"] = load(aw_sb, a["aw"].rearrange("p (k n) -> p k n", k=4), "aw")
            ffn_in["b"] = load(bcat_sb, a["bcat"], "bcat")
            ffn_in["low"] = load(lowtri[:, :], a["lowtri"], "lowtri")

        s_mid, s_gt, s_ge = sem("ffn_mid"), sem("ffn_gate"), sem("ffn_exp")
        s_xf, s_mg, s_mT, s_mTs, s_dl = sem("ffn_xT"), sem("ffn_mg"), sem("ffn_mgT"), sem("ffn_mgTs"), sem("ffn_delta")

        def ffn_mid(hf, t, first=(), filler=()):
            mid, filler = mids[hf], list(filler)
            xn, xT = {}, {}

            def norm(c):
                xn[c] = ln_xn(4 * hf + c, t)
                xn_read[4 * hf + c] = xn[c][1]

            def turn(c):
                p, tt = ln_T(*xn[c])
                f = c % 2
                act.wait(tt, ptb_free[f])
                xT[c] = act.run(lambda e: e.activation(pTb[:, f, :], PB[p][:, :], ACT.Copy), s_xf)
                bank_free[p] = xT[c]

            def times(c):
                f = c % 2
                pe.wait(xT[c], ffn_in["aw"], bank_free[2], bank_free[3])
                for k in range(4):
                    tm = pe.run(lambda e, k=k: e.matmul(
                        mid[:, c, :], pTb[:, f, k * 128:(k + 1) * 128], aw_sb[:, k, :],
                        start=(k == 0), stop=(k == 3)), s_mid if k == 3 else None)
                ptb_free[f] = tm
                return tm

            norm(0)
            norm(1)
            for f in first:
                f()
            for c in range(4):
                turn(c)
                if c + 2 < 4:
                    norm(c + 2)
                if c:
                    times(c - 1)
                if filler:
                    filler.pop(0)()
            return times(3)

        def ffn_gates(hf, tm):
            mid = mids[hf]
            lg, g16, e16, gat, gs, midg = (small[hf][n] for n in ("lg", "g16", "e16", "gat", "gs", "midg"))
            dve.wait(tm, ffn_in["low"], q_free[1])
            lj = lg.unsqueeze(2).broadcast_to([128, 4, 4, 4])
            le = lg.unsqueeze(3).broadcast_to([128, 4, 4, 4])
            G4 = g16.rearrange("p i (e j) -> p i e j", e=4)
            E4 = e16.rearrange("p i (e j) -> p i e j", e=4)
            low = lowtri[:, :].unsqueeze(1).broadcast_to([128, 4, 16])

            def chain(fs, s):
                for f in fs:
                    t = dve.run(f, s)
                    dve.wait(t)
                return t

            t = chain([
                lambda e: e.tensor_copy(lg, mid[:, :, 64:68]),
                lambda e: e.tensor_tensor(G4, lj, le, ALU.is_gt),
                lambda e: e.tensor_tensor(E4, lj, le, ALU.is_equal),
                lambda e: e.tensor_tensor(e16, e16, low, ALU.mult),
                lambda e: e.tensor_tensor(g16, g16, e16, ALU.add),
                lambda e: e.tensor_reduce(gat, G4, X, ALU.add),
                lambda e: e.tensor_scalar(gat, gat, 2.0, None, ALU.is_lt),
                lambda e: e.tensor_reduce(gs[:, 0, :], lg, X, ALU.max),
                lambda e: e.tensor_tensor(lg, lg, gs[:, 0, :].unsqueeze(2).broadcast_to([128, 4, 4]), ALU.subtract),
            ], s_gt)
            act.wait(t)
            t = act.run(lambda e: e.activation(lg, lg, ACT.Exp), s_ge)
            dve.wait(t)
            chain([
                lambda e: e.tensor_tensor(gat, gat, lg, ALU.mult),
                lambda e: e.tensor_reduce(gs[:, 1, :], gat, X, ALU.add),
                lambda e: e.reciprocal(gs[:, 2, :], gs[:, 1, :]),
                lambda e: e.scalar_tensor_tensor(
                    gat, gat, 4.0, gs[:, 2, :].unsqueeze(2).broadcast_to([128, 4, 4]), ALU.mult, ALU.mult),
            ], s_gt)
            for c in range(4):
                tg = dve.run(lambda e, c=c: e.tensor_tensor(
                    midg[:, c, :].rearrange("p (e r) -> p e r", e=4),
                    mid[:, c, 0:64].rearrange("p (e r) -> p e r", e=4),
                    gat[:, c, :].unsqueeze(2).broadcast_to([128, 4, 16]), ALU.mult), s_mg)
            return tg

        def ffn_delta(hf, tg, filler=()):
            midg = small[hf]["midg"]
            f = hf
            pm = next_bank()
            pe.wait(tg)
            for c in range(4):
                tt = pe.run(lambda e, c=c: e.transpose(PB[pm][0:64, c * 128:(c + 1) * 128], midg[:, c, :], ident[:, :]),
                            s_mT if c == 3 else None)
            act.wait(tt, ptb_free[f])
            tp = act.run(lambda e: e.activation(pTb[0:64, f, :], PB[pm][0:64, :], ACT.Copy), s_mTs)
            bank_free[pm] = tp
            for fill in filler:
                fill()
            for c in range(4):
                i = 4 * hf + c
                p = next_bank()
                pe.wait(tp, ffn_in["b"])
                td = pe.run(lambda e, c=c, p=p: e.matmul(PB[p][:, :], pTb[0:64, f, c * 128:(c + 1) * 128],
                                                         bcat_sb, start=True, stop=True), s_dl)
                dve.wait(td, x_ready[i], xn_read[i])
                tx = dve.run(lambda e, i=i, p=p: e.tensor_tensor(xs[:, i, :], xs[:, i, :], PB[p][:, :], ALU.add), s_x)
                bank_free[p] = tx
                x_ready[i] = tx
            ptb_free[f] = td
            return td

        mids = [bank[:, 0:272].rearrange("p (i n) -> p i n", i=4) for bank in (PS, PT)]

        w1k_tok, w1k_home = {}, {}

        def load_wk1(m, c):
            w1k_home[m] = c
            hi, lo, free = ((WKh[:, :], WKl[:, :], wk_free[0]), (WOh[:, 1, :], WOl[:, 1, :], wo_free[1]))[c]
            w1k_tok[m] = split_weight(a["wk1"][m], 128, 512, hi, lo, free)

        wv1_home = [(WVh[:, 0:384], WVl[:, 0:384]), (WVh[:, 512:896], WVl[:, 512:896]),
                    (WOh[:, 2, 0:384], WOl[:, 2, 0:384]), (WOh[:, 0, 0:384], WOl[:, 0, 0:384])]
        wv1_tok = []

        def load_wv1(k):
            hi, lo = wv1_home[k]
            wv1_tok.extend(split_weight(a["wv1"][:, 384 * k:384 * k + 384], 128, 384, hi, lo,
                                        (wv_free[0], wv_free[0], wo_free[2], wo_free[0])[k]))

        wq1_tok, wo1_tok = {}, {}

        def load_wq1(j, m):
            wq1_tok[(j, m)] = split_weight(a["wq1"][3 * j + m], 128, 512, WQh[:, m, :], WQl[:, m, :], wq_free[m])

        wo1_home = [(WOh[:, c, :], WOl[:, c, :]) for c in range(3)] + [
            (WVh[:, c:c + 512], WVl[:, c:c + 512]) for c in (0, 512)]
        wo1_free = [None] * 5

        def load_wo1(j, m):
            c = (3 * j + m) % 5
            hi, lo = wo1_home[c]
            r0 = 384 * j + 128 * m
            wo1_tok[(j, m)] = split_weight(a["wo1"][r0:r0 + 128, :], 128, 512, hi, lo, wo1_free[c])

        s_k1, s_v1 = sem("k1_sb"), sem("v1_sb")
        PACK = [[(0, 96, 0, 0), (96, 32, 1, 64)], [(0, 64, 1, 0), (64, 64, 2, 0)], [(0, 96, 3, 0), (96, 32, 2, 64)]]

        k1_ready, k1_done = {}, {}

        def k1_tile(m, w, hf):
            hi, lo = ((WKh, WKl), (WOh[:, 1], WOl[:, 1]))[w1k_home[m]]
            p = next_bank()
            pe.wait(w1k_tok[m], ctx_ready)
            if w:
                pe.wait(xn_ready[4 * hf + 3])
            b = slice(512 * hf, 512 * hf + 512)
            t = mm3(PB[p][:, :], [(hi[:, k * 128:(k + 1) * 128], lo[:, k * 128:(k + 1) * 128],
                                   HTh[w][:, k, b], HTl[w][:, k, b]) for k in range(4)], s_mm)
            if w1k_home[m] == 0:
                wk_free[0] = t
            act.wait(t)
            for r0, n, h, d0 in PACK[m]:
                src = PB[p][r0:r0 + n, :].rearrange("p (a r t) -> p a r t", a=4, r=2)
                dst = K1[h][d0:d0 + n].rearrange("p (a q t) -> p a q t", a=8, q=4)[:, 4 * hf:4 * hf + 4]
                dst = dst[:, :, 1:3, :] if w else dst[:, :, 0:4:3, :]
                tk = act.run(lambda e, dst=dst, src=src: e.activation(dst, src, ACT.Copy), s_k1)
                k1_ready[(h, w, hf)] = tk
            bank_free[p] = tk

        v1_ready = {}

        def v1_tile(w, i):
            p = next_bank()
            pe.wait(wv1_tok, ctx_ready)
            if w:
                pe.wait(xn_ready[i])
            b = slice(128 * i, 128 * i + 128)
            t = mm3(PB[p][:, 0:384], [(HTh[w][:, k, b], HTl[w][:, k, b],
                                       wv1_home[k][0], wv1_home[k][1]) for k in range(4)], s_mm)
            for c in range(5):
                wo1_free[c] = t
            act.wait(t)
            for r in range(2):
                at = 64 * (w ^ r)
                dst = V1[r][at:at + 64, :, 128 * i:128 * i + 96]
                src = PB[p][64 * r:64 * r + 64, 0:384].rearrange("p (j d) -> p j d", j=4)
                tv = act.run(lambda e, dst=dst, src=src: e.activation(dst, src, ACT.Copy), s_v1)
                v1_ready[(w, 2 * i + r)] = tv
            bank_free[p] = tv

        q1_ready = {}
        seam_done = [None]

        def stage_a1(g):
            j, hf = g // 2, g % 2
            b = slice(512 * hf, 512 * hf + 512)
            done = 0
            for m in range(3):
                p = next_bank()
                held.append(p)
                pe.wait(wq1_tok[(j, m)], xn_ready[4 * hf + 3])
                for k in range(4):
                    w = slice(k * 128, (k + 1) * 128)
                    for A, B in ((WQh, HTh), (WQh, HTl), (WQl, HTh)):
                        if done and done % 9 == 0:
                            yield
                        A, B, first, last = A[:, m, w], B[1][:, k, b], done % 12 == 0, done % 12 == 11
                        t = pe.run(lambda e, p=p, A=A, B=B, first=first, last=last: e.matmul(
                            PB[p][:, :], A, B, start=first, stop=last), s_mm if last else None)
                        done += 1
                wq_free[m] = t
                act.wait(t, q_free[g % 2], seam_done[0])
                for r0, n, h, d0 in PACK[m]:
                    dst = qb[d0:d0 + n, g % 2, 1024 * (h // 2):1024 * (h // 2) + 1024].rearrange(
                        "p (b n t) -> p n b t", b=8, n=2)[:, h % 2]
                    src = PB[p][r0:r0 + n, :].rearrange("p (b t) -> p b t", b=8)
                    tq = act.run(lambda e, dst=dst, src=src: e.activation(dst, src, ACT.Copy, scale=SC1), s_q1)
                held.remove(p)
                bank_free[p] = tq
                q1_ready[g] = tq
                if g % 2 == 1 and j + 1 < 4:
                    load_wq1(j + 1, m)

        def stage_b1(s):
            j, qd, pr = s // 8, s % 8 // 2, s % 2
            g = 2 * j + qd // 2
            e2 = s % 2
            pe.wait(bank_free[2], q1_ready[g], k1_ready[(j, 0, qd // 2)], k1_ready[(j, 1, qd // 2)])
            for bb in range(4):
                b8, b = 4 * (qd % 2) + bb, 4 * qd + bb
                t = pe.run(lambda e, bb=bb, b8=b8, b=b: e.matmul(
                    PS[:, bb * 128:(bb + 1) * 128],
                    qb[0:96, g % 2, 1024 * pr + b8 * 128:1024 * pr + (b8 + 1) * 128],
                    K1[j][:, b * 128:(b + 1) * 128], start=True, stop=True), s_sc if bb == 3 else None)
            q_free[g % 2] = t
            k1_done[j] = t
            mx, rs = sm[:, e2, 0, 0:4], sm[:, e2, 0, 4:8]
            rr = sm[:, e2, 1, 0:4]
            E3 = Eb[:, e2, :].rearrange("p (b t) -> p b t", b=4)
            dve.wait(t, rr_free[e2])
            t1 = dve.run(lambda e: e.tensor_reduce(mx, PS[:, :].rearrange("p (b t) -> p b t", b=4), X, ALU.max,
                                                   negate=True), s_max)
            act.wait(t1, eb_free[e2])
            for bb in range(4):
                t2 = act.run(lambda e, bb=bb: e.activation(
                    Eb[:, e2, bb * 128:(bb + 1) * 128], PS[:, bb * 128:(bb + 1) * 128], ACT.Exp,
                    bias=mx[:, bb:bb + 1], accum_out=rs[:, bb:bb + 1]), s_exp)
            bank_free[2] = t2
            dve.wait(t2)
            t5 = dve.run(lambda e: e.reciprocal(rr, rs), s_rec)
            dve.wait(t5)
            t6 = dve.run(lambda e: e.tensor_tensor(E3, E3, rr.unsqueeze(2).broadcast_to([128, 4, 128]), ALU.mult), s_nrm)
            rr_free[e2] = t6
            p_ready[s] = t6

        Ohp, Olp = (O[:, :, :, :].rearrange("p s n t -> p s (n t)") for O in (Oh, Ol))
        o1_free = [None, None]
        o1_ready = {}

        def stage_d1(s):
            j, qd, pr = s // 8, s % 8 // 2, s % 2
            e2, os = s % 2, (s // 2) % 2
            pe.wait(pt_ready[s], bank_free[4 + e2])
            for bb in range(4):
                b = 4 * qd + bb
                pe.wait(v1_ready[(1, b)])
                t = pe.run(lambda e, bb=bb, b=b: e.matmul(
                    PA[e2][0:96, bb * 128:(bb + 1) * 128], V1[b % 2][:, j, 128 * (b // 2):128 * (b // 2) + 96],
                    pTb[:, e2, bb * 128:(bb + 1) * 128], start=True, stop=True), s_av if bb == 3 else None)
            ptb_free[e2] = t
            act.wait(t, o1_free[os])
            moves = []
            for m in range(3):
                for r0, n, h, d0 in PACK[m]:
                    if h // 2 == pr:
                        src = PA[e2][d0:d0 + n, :].rearrange("p (b n t) -> p n b t", b=4, n=2)[:, h % 2]
                        dh, dl = (O[r0:r0 + n, os, 256 * m:256 * m + 256].rearrange("p (b t) -> p b t", b=4)
                                  for O in (Ohp, Olp))
                        th = act.run(lambda e, dh=dh, src=src: e.activation(dh, src, ACT.Copy), s_oh)
                        moves.append((src, dh, dl, th))
            dve.wait(o1_free[os], th)
            for src, dh, dl, _ in moves:
                tl = dve.run(lambda e, dh=dh, dl=dl, src=src: e.tensor_tensor(dl, src, dh.bitcast(f32), ALU.subtract), s_ol)
            bank_free[4 + e2] = tl
            o1_ready[s] = tl

        def stage_e1(j, i):
            qd, c = i // 2, i % 2
            s = 8 * j + 2 * qd
            os = (s // 2) % 2
            p = next_bank()
            pe.wait(o1_ready[s + 1], wo1_tok[(j, 1)])
            homes = [wo1_home[(3 * j + m) % 5] for m in range(3)]
            t = mm3(PB[p][:, :], [(Ohp[:, os, 256 * m + 128 * c:256 * m + 128 * c + 128],
                                   Olp[:, os, 256 * m + 128 * c:256 * m + 128 * c + 128],
                                   homes[m][0], homes[m][1], wo1_tok[(j, m)]) for m in range(3)], s_wo)
            dve.wait(t, x_ready[i], xn_read[i])
            tx = dve.run(lambda e: e.tensor_tensor(xs[:, i, :], xs[:, i, :], PB[p][:, :], ALU.add), s_x)
            bank_free[p] = tx
            x_ready[i] = tx
            o1_free[os] = t
            for m in range(3):
                wo1_free[(3 * j + m) % 5] = t

        s_q1, s_max = sem("q1_sb"), sem("rowmax")
        for b in (2, 3, 4, 5):
            ring.remove(b)
        NS = 32
        for it in range(NS + 2):
            if 0 <= it - 1 < NS:
                stage_b(it - 1)
            if it % 4 == 0 and it // 4 + 1 < 8:
                wk_tok = load_wk(it // 4 + 1)
            if it % 8 == 1 and it // 8 + 1 < 4:
                wv_tok = load_wv(it // 8 + 1)
            if it % 2 == 0 and it // 2 + 1 < 16:
                load_wq(it + 2)
            if it % 2 == 1 and it < NS:
                load_wo(it - 1)
            if 0 < it < NS:
                stage_a(it)
            if it == NS + 1:
                k1_tile(0, 0, 0)
            if 0 <= it - 2 < NS:
                stage_d(it - 2)
            if it % 2 == 1 and it + 2 < 32:
                load_wq(it + 2)
            if 0 <= it - 3 < NS:
                stage_e(it - 3)
            if it % 2 == 0 and 2 <= it <= NS:
                load_wo(it - 1)
            if it % 4 in (1, 2) and it // 4 + 1 < 8:
                k_half(it // 4 + 1, it % 4 - 1, wk_tok)
            if 3 <= it % 8 <= 6 and it // 8 + 1 < 4:
                for i in range(2):
                    v_tile(it // 8 + 1, 2 * (it % 8 - 3) + i, wv_tok)
            if 0 <= it - 1 < NS:
                stage_c(it - 1)
            if it == NS - 2:
                load_wk1(0, 0)
            if it == NS - 1:
                load_wv1(0)
                load_wv1(1)
            if it == NS:
                load_wq1(0, 0)
                load_wq1(0, 1)
            if it == NS + 1:
                load_wv1(2)
                load_wq1(0, 2)
                load_ffn()

        lo, hi = range(0, 4), range(4, 8)
        t_lo = ln_prep(lo, x_ready)
        ring[0:0] = [4, 5]
        stage_e(NS - 1)
        t_hi = ln_prep(hi, x_ready)
        t_m0 = ffn_mid(0, t_lo, [lambda: k1_tile(0, 0, 1)], [lambda: load_wk1(1, 1)])
        load_wk1(2, 0)
        load_wv1(3)
        t_g0 = ffn_gates(0, t_m0)
        t_m1 = ffn_mid(1, t_hi, [lambda: k1_tile(1, 0, 0)])
        t_g1 = ffn_gates(1, t_m1)
        ffn_delta(0, t_g0, [lambda: k1_tile(1, 0, 1)])
        t_ln = ln_prep(lo, x_ready)
        k1_tile(2, 0, 0)
        xn_ready = {}
        seam_done[0] = ffn_delta(1, t_g1, [lambda: k1_tile(2, 0, 1)])
        load_wk1(0, 0)
        bank_free[2] = t_g0
        bank_free[3] = t_g1
        ring[0:0] = [2, 3]
        ln_apply(lo, t_ln, None, xn_ready, [lambda i=i: v1_tile(0, i) for i in range(4)])
        t_ln = ln_prep(hi, x_ready)
        for _ in stage_a1(0):
            pass
        ln_apply(hi, t_ln, None, xn_ready, [lambda i=i: v1_tile(0, i) for i in range(5, 8)], [lambda: v1_tile(0, 4)])
        for hf in range(2):
            k1_tile(0, 1, hf)
        load_wk1(1, 0)
        for i in range(5):
            v1_tile(1, i)

        weff_ready = []
        s_wc, s_bw, s_we, s_wa, s_wh, s_wl = (sem("w_col"), sem("b_scaled"), sem("weff_ps"), sem("weff_sum"),
                                              sem("weff_hi"), sem("weff_lo"))

        weff_in = {}
        we_home = [(WQh[:, m, :], WQl[:, m, :]) for m in range(3)] + [(WKh[:, :], WKl[:, :])]

        def weff_load():
            sp.wait(k1_done[0])
            weff_in["w"] = load(w1T, a["w1"].rearrange("p (k n) -> p k n", k=4), "w1")
            t_c = load(coef[:, 0:2], a["coef"], "coef")
            t_s = load(coef[:, 2:4], a["scl"], "scl")
            weff_in["a"] = [load(ab_sb[:, c, :], a["a1"][c], f"a1_{c}") for c in range(2)]
            got = [load(ab_sb[:, 2 + c, :], a["bf1"][c], f"bf1_{c}") for c in range(2)]
            dve.wait(t_c, t_s)
            t = dve.run(lambda e: e.tensor_tensor(wcol[:, :], coef[:, 0:2], coef[:, 2:4], ALU.mult), s_wc)
            pool.wait(t)
            for c in range(2):
                pool.wait(got[c])
                weff_in["b"] = pool.run(lambda e, c=c: e.tensor_scalar(
                    ab_sb[:, 2 + c, :], ab_sb[:, 2 + c, :], wcol[:, c:c + 1], None, ALU.mult), s_bw)

        def weff(m, later=None):
            p = next_bank()
            pe.wait(weff_in["b"], weff_in["a"])
            for c in range(2):
                t = pe.run(lambda e, c=c: e.matmul(
                    PB[p][:, :], ab_sb[:, c, m * 128:(m + 1) * 128], ab_sb[:, 2 + c, :],
                    start=(c == 0), stop=(c == 1)), s_we if c == 1 else None)
            src = w1T[:, m, :]
            dve.wait(t, weff_in["w"])
            ta = dve.run(lambda e: e.tensor_tensor(src, src, PB[p][:, :], ALU.add), s_wa)
            bank_free[p] = ta
            (dh, dl), free = we_home[m], wq_free[m] if m < 3 else wk_free[0]

            def split():
                act.wait(ta, free)
                th = act.run(lambda e: e.activation(dh, src, ACT.Copy), s_wh)
                pool.wait(ta, th, free)
                weff_ready[:] = [pool.run(lambda e: e.tensor_tensor(dl, src, dh.bitcast(f32), ALU.subtract), s_wl)]

            if later is None:
                split()
            else:
                later.append(split)

        s_xb, s_y, s_out = sem("x_bias"), sem("y_ps"), sem("out")
        fin_ready = {}
        fin = {}

        def load_bias():
            (i, tok), = stage_load([(a["bias"], 128, 512)])
            fin["slot"], fin["bias"] = i, tok

        def add_bias(tiles):
            biasb = stage[:, fin["slot"], :]
            for i in tiles:
                pool.wait(fin["bias"], xn_read[i], x_ready[i])
                fin[i] = pool.run(lambda e, i=i: e.tensor_tensor(xs[:, i, :], xs[:, i, :], biasb, ALU.add), s_xb)

        def dense(i):
            p = next_bank()
            pe.wait(fin_ready[i], weff_ready)
            b = slice(128 * i, 128 * i + 128)
            t = mm3(PB[p][:, :], [(HTh[1][:, k, b], HTl[1][:, k, b], *we_home[k])
                                  for k in range(4)], s_y)
            dve.wait(t, fin[i])
            ty = dve.run(lambda e: e.tensor_tensor(xs[:, i, :], xs[:, i, :], PB[p][:, :], ALU.add), s_x)
            bank_free[p] = ty
            sp.wait(ty)
            fin["out"] = sp.run(lambda e: e.dma_start(out[i * 128:(i + 1) * 128, :], xs[:, i, :]), s_out, 16)

        for b in (2, 3, 4, 5):
            ring.remove(b)
        N1 = 32
        k1_plan = {4: (1, 1, 0), 8: (1, 1, 1), 12: (2, 1, 0), 16: (2, 1, 1)}
        st4 = []
        for it in range(N1 + 1):
            if 0 <= it - 2:
                stage_c(it - 2)
            if 0 <= it - 1 < N1:
                stage_b1(it - 1)
            if it < 3:
                v1_tile(1, 5 + it)
            if it in (3, 8, 16, 24):
                load_wo1(it // 8, 0)
                load_wo1(it // 8, 1)
            if 1 <= it <= 28:
                if it % 4 == 1:
                    queries = stage_a1((it + 3) // 4)
                next(queries, None)
            if it in k1_plan:
                k1_tile(*k1_plan[it])
                if it == 8:
                    load_wk1(2, 0)
            if 0 <= it - 5:
                stage_e1((it - 5) // 8, (it - 5) % 8)
            if it == N1 - 4:
                load_wo1(3, 2)
            elif it % 8 == 4:
                load_wo1(it // 8, 2)
            if 0 <= it - 2:
                stage_d1(it - 2)
            if it == N1 - 6:
                weff_load()
            if it in (28, 30, 32):
                weff((it - 28) // 2)
            if N1 - 2 <= it:
                st4.append(ln_stats(it - (N1 - 2), x_ready[it - (N1 - 2)]))

        ring[0:0] = [2]
        stage_e1(3, 4)
        stage_c(N1 - 1)
        t_lo = ln_prep(lo, x_ready, [q_free[0], q_free[1]], st4)
        stage_d1(N1 - 1)
        ring[0:0] = [3]
        ring += [4, 5]
        later = []
        weff(3, later)
        load_bias()
        stage_e1(3, 5)
        ln_apply(lo, t_lo, None, fin_ready, [later[0], lambda: stage_e1(3, 6), lambda: stage_e1(3, 7)])
        t_hi = ln_prep(hi, x_ready)
        add_bias(lo)
        for i in range(3):
            dense(i)
        ln_apply(hi, t_hi, None, fin_ready, [None, lambda: dense(3)])
        add_bias(hi)
        for i in hi:
            dense(i)

        sp.wait(fin["out"])

        block = ctx.enter_context(nc.Block())

        @block.sync
        def _(e):
            sp.emit(e)

        @block.scalar
        def _(e):
            act.emit(e)

        @block.gpsimd
        def _(e):
            pool.emit(e)

        @block.vector
        def _(e):
            dve.emit(e)

        @block.tensor
        def _(e):
            pe.emit(e)


def kernel(**inputs):
    import numpy as np
    import concourse.bacc as bacc
    from concourse.bass_utils import run_bass_kernel_spmd as run

    g = {k: np.asarray(v) for k, v in inputs.items()}
    half = np.float32(1.0) / np.float32(10000.0) ** (np.arange(0, 128, 2, dtype=np.float32) / np.float32(128))
    phase = np.arange(64, dtype=np.float32)[None, :] * half.astype(np.float32)[:, None]
    cos, sin = np.cos(phase), np.sin(phase)
    rope = np.concatenate([np.concatenate([cos, cos], 0), np.concatenate([sin, -sin], 0)], 1)
    low = np.array([[1.0 if j < e else 0.0 for j in range(4)] for e in range(4)], np.float32).reshape(1, 16)
    pk = lambda w: w.reshape(4, 128, -1).transpose(1, 0, 2)
    heads = lambda w, n: w.reshape(4, 128, n, -1).transpose(2, 1, 0, 3).reshape(n, 128, -1)
    rows = np.concatenate([96 * h + np.arange(d, d + n) for h, d, n in (
        (0, 0, 96), (1, 64, 32), (1, 0, 64), (2, 0, 64), (3, 0, 96), (2, 64, 32))])
    packed = lambda w: w.reshape(-1, 384, 512)[:, rows].reshape(-1, 512)
    a = {
        "x": g["x"].reshape(1024, 512),
        "ctxT": g["ctx_4096"].reshape(1024, 512).T,
        "mask": np.concatenate([g["mask_1x1xSxS2_bk0"].reshape(64, 64)] * 2, 0).view(np.int32),
        "rope": rope.astype(np.float32),
        "ident": np.eye(128, dtype=np.float32),
        "lowtri": np.broadcast_to(low, (128, 16)),
        "wq0": heads(g["L0_xattn_Wq"], 32),
        "wk0": heads(g["L0_xattn_Wk"], 8),
        "wv0": heads(g["L0_xattn_Wv"], 4),
        "wo0": g["L0_xattn_Wo"],
        "aw": pk(np.concatenate([g["L0_ffn_A"].reshape(64, 512), g["L0_ffn_Wr"]], 0).T).reshape(128, 272),
        "bcat": g["L0_ffn_B"].transpose(0, 2, 1).reshape(64, 512),
        "wq1": heads(packed(g["L1_xattn_Wq"]).T, 12),
        "wk1": heads(packed(g["L1_xattn_Wk"]).T, 3),
        "wv1": pk(g["L1_xattn_Wv"].T).reshape(128, 1536),
        "wo1": packed(g["L1_xattn_Wo"].T),
        "w1": pk(g["L1_ffn_W"].T).reshape(128, 2048),
        "a1": g["L1_ffn_A"].reshape(2, 128, 512),
        "bf1": g["L1_ffn_Bf"].transpose(0, 2, 1).reshape(2, 128, 512),
        "coef": np.repeat(g["L1_ffn_coeffs"], 16).reshape(2, 128).T,
        "scl": np.repeat(g["L1_ffn_scales"], 16).reshape(2, 128).T,
        "bias": np.broadcast_to(g["L1_ffn_bias"][None, :], (128, 512)),
    }
    nc = bacc.Bacc("TRN2", target_bir_lowering=False, num_devices=1)
    arrays, aps = {}, {}
    for name in INS:
        v = np.ascontiguousarray(a[name])
        arrays["in_" + name] = v
        aps[name] = nc.dram_tensor("in_" + name, v.shape, mybir.dt.from_np(v.dtype), kind="ExternalInput").ap()
    out = nc.dram_tensor("out_0", (1024, 512), mybir.dt.float32, kind="ExternalOutput").ap()
    program(nc, aps, out)
    r = run(nc, [arrays], core_ids=[0])
    return np.asarray(r.results[0]["out_0"]).reshape(16, 64, 512)
```
